# Optimizing a Trainium2 kernel written in Bass

```python
import numpy as np
import jax
import jax.numpy as jnp

def _softmax(x, axis=-1):
    return jax.nn.softmax(x, axis=axis)

def _gelu(x):
    return jax.nn.gelu(x, approximate=True)

def _silu(x):
    return jax.nn.silu(x)

def _sigmoid(x):
    return jax.nn.sigmoid(x)

def _layernorm(x, axis=-1, eps=1e-05):
    m = jnp.mean(x, axis=axis, keepdims=True)
    v = jnp.var(x, axis=axis, keepdims=True)
    return (x - m) / jnp.sqrt(v + eps)

def _scatter_add(tgt, idx, src, axis=0):
    return tgt.at[idx].add(src)

def _segment_sum(src, seg, n):
    return jax.ops.segment_sum(src, seg, n)
kernel_name = 'mk_flamingo_gated_d1_seqx_r4_a84ed0'

def setup_inputs(seed: int=0):
    np.random.seed(seed)
    _w = jnp.asarray

    def _rec_inputs():
        import jax
        import jax.numpy as jnp
        _rk = jax.random.key(seed)
        x = -0.0003929 + 0.9999 * jax.random.normal(jax.random.fold_in(_rk, 1), (1, 2048, 256), jnp.float32)
        _lenS = 2048 - jax.random.randint(jax.random.fold_in(_rk, 7), (1,), 0, max(1, 2048 // 4) + 1, jnp.int32)
        _lenS2 = 1601 - jax.random.randint(jax.random.fold_in(_rk, 8), (1,), 0, max(1, 1601 // 4) + 1, jnp.int32)
        _ctx_768P = jax.random.normal(jax.random.fold_in(_rk, 11), (1, 16, 192), jnp.float32)
        _ctx_768c = jax.random.dirichlet(jax.random.fold_in(_rk, 511), 0.3 * jnp.ones((16,), jnp.float32), (1, 1601))
        _ctx_768t = jnp.einsum('bsk,bkd->bsd', _ctx_768c, _ctx_768P)
        _ctx_768t = _ctx_768t * jax.lax.rsqrt(jnp.mean(jnp.square(_ctx_768t)) + 1e-12) * 0.953939
        ctx_768 = -0.00055796 + 0.999787 * (_ctx_768t + 0.3 * jax.random.normal(jax.random.fold_in(_rk, 611), (1, 1601, 192), jnp.float32))
        _g = jax.random.normal(jax.random.fold_in(_rk, 9001), (2, 1), jnp.float32)
        _g = jnp.sign(_g) * jnp.maximum(jnp.abs(_g), 1.0) + (_g == 0) * 1.0
        g_xattn = _g[0]
        g_ffn = _g[1]
        return (x, ctx_768, g_xattn, g_ffn)
    x, ctx_768, g_xattn, g_ffn = _rec_inputs()

    def _L0_xattn_setup():
        import jax, jax.numpy as jnp
        import numpy as np
        IMAGE_DIM = 256
        TEXT_DIM = 192
        NUM_HEADS = 16
        HEAD_DIM = IMAGE_DIM // NUM_HEADS
        key = jax.random.key(seed)
        ks = jax.random.split(key, 14)
        B, N, M = (4, 1024, 128)
        s_img = 1.0 / np.sqrt(IMAGE_DIM)
        s_txt = 1.0 / np.sqrt(TEXT_DIM)
        s_ff = 1.0 / np.sqrt(2 * IMAGE_DIM)
        return {'x': jax.random.normal(ks[0], (B, N, IMAGE_DIM), jnp.float32), 'y': jax.random.normal(ks[1], (B, M, TEXT_DIM), jnp.float32), 'Wq': jax.random.normal(ks[2], (IMAGE_DIM, IMAGE_DIM), jnp.float32) * s_img, 'bq': jax.random.normal(ks[3], (IMAGE_DIM,), jnp.float32) * s_img, 'Wk': jax.random.normal(ks[4], (TEXT_DIM, IMAGE_DIM), jnp.float32) * s_txt, 'bk': jax.random.normal(ks[5], (IMAGE_DIM,), jnp.float32) * s_txt, 'Wv': jax.random.normal(ks[6], (TEXT_DIM, IMAGE_DIM), jnp.float32) * s_txt, 'bv': jax.random.normal(ks[7], (IMAGE_DIM,), jnp.float32) * s_txt, 'W1': jax.random.normal(ks[8], (IMAGE_DIM, 2 * IMAGE_DIM), jnp.float32) * s_img, 'b1': jax.random.normal(ks[9], (2 * IMAGE_DIM,), jnp.float32) * s_img, 'W2': jax.random.normal(ks[10], (2 * IMAGE_DIM, IMAGE_DIM), jnp.float32) * s_ff, 'b2': jax.random.normal(ks[11], (IMAGE_DIM,), jnp.float32) * s_ff}
    _L0_xattn_all = _L0_xattn_setup()
    _L0_xattn_in = {k: v for k, v in _L0_xattn_all.items() if k in ('Wq', 'bq', 'Wk', 'bk', 'Wv', 'bv', 'W1', 'b1', 'W2', 'b2')}
    del _L0_xattn_all

    def _L0_ffn_setup():
        import jax, jax.numpy as jnp
        import numpy as np
        K = 64
        key = jax.random.key(seed)
        ks = jax.random.split(key, 9)
        B, S, D, O, E = (8, 512, 256, 256, 16)

        def xavier(k_, shape):
            fan_in, fan_out = (shape[-2], shape[-1])
            lim = (6.0 / (fan_in + fan_out)) ** 0.5
            return jax.random.uniform(k_, shape, jnp.float32, -lim, lim)
        return {'x': jax.random.normal(ks[0], (B, S, D), jnp.float32), 'Wg': xavier(ks[1], (D, E)), 'bg': jnp.zeros((E,), jnp.float32), 'w1': xavier(ks[2], (E, D, O)), 'b1': xavier(ks[3], (E, 1)), 'w2': xavier(ks[4], (E, O, O)), 'b2': xavier(ks[5], (E, 1)), 'w3': xavier(ks[6], (E, O, O)), 'b3': xavier(ks[7], (E, 1))}
    _L0_ffn_all = _L0_ffn_setup()
    _L0_ffn_in = {k: v for k, v in _L0_ffn_all.items() if k in ('Wg', 'bg', 'w1', 'b1', 'w2', 'b2', 'w3', 'b3')}
    del _L0_ffn_all
    return {'x': x, 'ctx_768': ctx_768, 'g_xattn': g_xattn, 'g_ffn': g_ffn, 'L0_xattn_Wq': _L0_xattn_in['Wq'], 'L0_xattn_bq': _L0_xattn_in['bq'], 'L0_xattn_Wk': _L0_xattn_in['Wk'], 'L0_xattn_bk': _L0_xattn_in['bk'], 'L0_xattn_Wv': _L0_xattn_in['Wv'], 'L0_xattn_bv': _L0_xattn_in['bv'], 'L0_xattn_W1': _L0_xattn_in['W1'], 'L0_xattn_b1': _L0_xattn_in['b1'], 'L0_xattn_W2': _L0_xattn_in['W2'], 'L0_xattn_b2': _L0_xattn_in['b2'], 'L0_ffn_Wg': _L0_ffn_in['Wg'], 'L0_ffn_bg': _L0_ffn_in['bg'], 'L0_ffn_w1': _L0_ffn_in['w1'], 'L0_ffn_b1': _L0_ffn_in['b1'], 'L0_ffn_w2': _L0_ffn_in['w2'], 'L0_ffn_b2': _L0_ffn_in['b2'], 'L0_ffn_w3': _L0_ffn_in['w3'], 'L0_ffn_b3': _L0_ffn_in['b3']}

def reference(x, ctx_768, g_xattn, g_ffn, L0_xattn_Wq, L0_xattn_bq, L0_xattn_Wk, L0_xattn_bk, L0_xattn_Wv, L0_xattn_bv, L0_xattn_W1, L0_xattn_b1, L0_xattn_W2, L0_xattn_b2, L0_ffn_Wg, L0_ffn_bg, L0_ffn_w1, L0_ffn_b1, L0_ffn_w2, L0_ffn_b2, L0_ffn_w3, L0_ffn_b3):
    import jax
    import jax.numpy as jnp

    def _L0_xattn_ref(x, y, Wq, bq, Wk, bk, Wv, bv, W1, b1, W2, b2):
        import jax, jax.numpy as jnp
        import numpy as np
        IMAGE_DIM = 256
        TEXT_DIM = 192
        NUM_HEADS = 16
        HEAD_DIM = IMAGE_DIM // NUM_HEADS
        B, N, _ = x.shape
        M = y.shape[1]
        q = (x @ Wq + bq).reshape(B, N, NUM_HEADS, HEAD_DIM)
        k = (y @ Wk + bk).reshape(B, M, NUM_HEADS, HEAD_DIM)
        v = (y @ Wv + bv).reshape(B, M, NUM_HEADS, HEAD_DIM)
        scale = 1.0 / np.sqrt(HEAD_DIM)
        scores = jnp.einsum('bnhd,bmhd->bhnm', q, k) * scale
        attn = jax.nn.softmax(scores, axis=-1)
        out = jnp.einsum('bhnm,bmhd->bnhd', attn, v).reshape(B, N, IMAGE_DIM)
        h = jax.nn.relu(out @ W1 + b1)
        return h @ W2 + b2

    def _L0_ffn_ref(x, Wg, bg, w1, b1, w2, b2, w3, b3):
        import jax, jax.numpy as jnp
        import numpy as np
        K = 64
        B, S, D = x.shape
        E, _, O = w1.shape
        logits = jnp.einsum('bsd,de->bse', x, Wg) + bg
        probs = jax.nn.softmax(logits, axis=-2)
        pv = jnp.transpose(probs, (0, 2, 1))
        vals, idx = jax.lax.top_k(pv, K)
        bidx = jnp.arange(B)[:, None, None]
        tok = x[bidx, idx]
        b1b = b1[None, :, None, :]
        b2b = b2[None, :, None, :]
        b3b = b3[None, :, None, :]
        h = jax.nn.relu(jnp.einsum('bekd,edo->beko', tok, w1) + b1b)
        h = jax.nn.relu(jnp.einsum('bekd,edo->beko', h, w2) + b2b)
        h = jnp.einsum('bekd,edo->beko', h, w3) + b3b
        out = h * vals[..., None]
        outputs = jnp.zeros((B, S, O), x.dtype).at[bidx, idx].add(out)
        return outputs
    x = x + jnp.tanh(g_xattn[0]) * _L0_xattn_ref(_layernorm(x, axis=-1), ctx_768, L0_xattn_Wq, L0_xattn_bq, L0_xattn_Wk, L0_xattn_bk, L0_xattn_Wv, L0_xattn_bv, L0_xattn_W1, L0_xattn_b1, L0_xattn_W2, L0_xattn_b2)
    x = x + jnp.tanh(g_ffn[0]) * _L0_ffn_ref(_layernorm(x, axis=-1), L0_ffn_Wg, L0_ffn_bg, L0_ffn_w1, L0_ffn_b1, L0_ffn_w2, L0_ffn_b2, L0_ffn_w3, L0_ffn_b3)
    return x

_drawn_inputs = setup_inputs


def setup_inputs(seed=0):
    import zlib

    import numpy as np

    out = dict(_drawn_inputs(seed))
    spreads = {'L0_ffn_bg': (0.0, 2.0)}
    factors = {'L0_xattn_bq': 8.0,
     'L0_xattn_bk': 64.0,
     'L0_ffn_Wg': 8.0,
     'L0_ffn_w1': 8.0,
     'L0_ffn_b1': 8.0,
     'L0_ffn_w2': 8.0,
     'L0_ffn_b2': 8.0,
     'L0_ffn_w3': 8.0,
     'L0_ffn_b3': 53.544}
    for name, (base, spread) in spreads.items():
        noise = np.random.default_rng([zlib.crc32(name.encode()), seed]).standard_normal(out[name].shape)
        drawn = base * np.exp(spread * noise) if base else spread * noise
        out[name] = jnp.asarray(drawn.astype(out[name].dtype))
    for name, factor in factors.items():
        out[name] = (out[name] * factor).astype(out[name].dtype)
    return out
```

```python
import concourse.bass as bass
from concourse import mybir
from contextlib import ExitStack

F32, BF16, U32, I32 = mybir.dt.float32, mybir.dt.bfloat16, mybir.dt.uint32, mybir.dt.int32
ALU, ACT, AX = mybir.AluOpType, mybir.ActivationFunctionType, mybir.AxisListType

T, D, C, S = 2048, 256, 192, 1601
H, DH = 16, 16
FF = 2 * D
EX, TOP = 16, 64
EPS = 1e-5
SCALE = 1.0 / DH ** 0.5

QB = 512
NB = T // QB
HG = 4
NG = H // HG
STEPS = NB * NG
QT = QB // 128
KT = -(-S // 128)
KLAST = S - (KT - 1) * 128
PAIRS = 2 * KT
KC = -(-S // 4)
CHUNKS = [(c * KC, min(KC, S - c * KC)) for c in range(4)]
QCHUNKS = HG * 4
ACH = QT * QCHUNKS
LEAD = 1
PARTS = 3 * DH * 2
HM = 8
CH = C // 2

PROJ = ([("k", 0, c, n) for c, n in CHUNKS] + [("q", 0, 0, QB)] + [("k", 1, c, n) for c, n in CHUNKS]
        + [("q", 1, 0, QB)] + [("q", m, b * QB, QB) for b in range(1, NB) for m in (0, 1)])
NPROJ = len(PROJ)
DVE_SPLITS = 5
STORES = {"k": 1, "q": 3}

MLP_UNITS = [(3, "bc0"), (4, "bc1"), (5, "w1_0"), (6, "w1_1"), (7, "w1_2"), (8, "w1_3"),
             (9, "w2_0"), (10, "w2_1"), (11, "w2_2"), (12, "w2_3")]
LN_UNITS = [(4, "tr0"), (5, "tr1"), (7, "lg")]
NEG_AT = 10


def plan(n):
    units = []
    if n >= NG:
        units += MLP_UNITS if n % NG == 0 else LN_UNITS if n % NG == 1 else []
    if n < STEPS - 1:
        units = units + [(NEG_AT, "neg")]
    return sorted(units, key=lambda u: u[0])


def spare_bank_order():
    order = [("neg", 0)]
    for n in range(STEPS):
        order += [("neg", n + 1) if u == "neg" else (u, n // NG - 1) for _, u in plan(n)]
    order += [(u, NB - 1) for _, u in MLP_UNITS + LN_UNITS]
    return {key: k for k, key in enumerate(order)}


ORDER = spare_bank_order()
USES_PER_BLOCK = NG + len(MLP_UNITS) + len(LN_UNITS)


class Step:

    def __init__(self, n0, r=None):
        self.n0, self.r, self.g = n0, r, n0 % NG

    def after(self, k):
        return Step(self.n0 + k, self.r)

    def count(self, per_step, plus=0):
        const = per_step * self.n0 + plus
        return const if self.r is None else self.r * (per_step * NG) + const

    def use(self, unit):
        k = ORDER[(unit, self.n0 if unit == "neg" else self.n0 // NG)]
        return k if self.r is None else self.r * USES_PER_BLOCK + k

    def block(self, plus=0, scale=1):
        const = (self.n0 // NG + plus) * scale
        return const if self.r is None else self.r * scale + const

    def halves(self, scale):
        const = self.n0 // 2 * scale
        return const if self.r is None else self.r * (NG // 2 * scale) + const


def wait(eng, sem, value):
    if not isinstance(value, int) or value > 0:
        eng.wait_ge(sem, value)


def run_steps(eng, step):
    for n in (0, 1):
        step(Step(n))
    with eng.Fori(0, NB - 1) as r:
        for n in range(2, 2 + NG):
            step(Step(n, r))
    for n in (STEPS - 2, STEPS - 1):
        step(Step(n))


def row_max_chunks(n0):
    out = []
    for q in range(QT):
        ahead, t = 1 + (q + LEAD) // QT, (q + LEAD) % QT
        if n0 + ahead < STEPS:
            out += [(ahead, t, h, c) for h in range(HG) for c in range(4)]
    return out


def flamingo(nc, x, ctx_t, wq, b_qk, wk, wv, bv, w1, b1, w2, b2, wg, bg, gates, ew, eb, out):
    es = ExitStack()
    with es:
        def sb(name, shape, dt):
            return es.enter_context(nc.sbuf_tensor(name, shape, dt))

        def pb(name, shape, dt):
            return es.enter_context(nc.psum_tensor(name, shape, dt))

        def sem(name):
            return es.enter_context(nc.semaphore(name))

        def dram(name, shape, dt):
            return nc.dram_tensor(name, shape, dt, kind="Internal").ap()

        region = sb("region", [128, 3 * EX * 2 * D], F32)
        used = [0]

        def carve(words):
            used[0] += words
            return region[:, used[0] - words:used[0]]

        k_rows = carve(H * S // 2).bitcast(BF16).rearrange("p (h s) -> p h s", h=H)
        q_rows = carve(H * QB // 2).bitcast(BF16).rearrange("p (g h n) -> p g h n", g=NG, h=HG)
        v_cols = carve(KT * H * (DH + 1)).rearrange("p (k h d) -> p k h d", k=KT, h=H)
        p_flat = carve(4 * 2 * QB)
        probs = p_flat.rearrange("p (s b n) -> p s b n", s=4, b=2)
        w_exp = region[:, :].rearrange("p (l e k o) -> p l e k o", l=3, e=EX, k=2)

        x_in = sb("x_in", [128, T // 128, D], F32)
        xn_t = sb("xn_t", [128, 2 * T], F32)
        xn_tv = xn_t[:, :].rearrange("p (k n) -> p k n", k=2)
        hidden = xn_t[:, 0:4 * QB].rearrange("p (m n) -> p m n", m=4)
        att_t = xn_t[:, 4 * QB:6 * QB].rearrange("p (k n) -> p k n", k=2)
        xn2_t = xn_t[:, 6 * QB:8 * QB].rearrange("p (k n) -> p k n", k=2)
        ctx_sb = sb("ctx_sb", [128, 2, S], F32)
        logits = ctx_sb[0:EX, :, :].rearrange("p k s -> p (k s)")[:, 0:T]
        wq_sb = sb("wq_sb", [128, 2, D], F32)
        wk_sb = sb("wk_sb", [CH, 2, D], F32)
        wv_sb = sb("wv_sb", [CH + 1, 2, D], F32)
        bqk = sb("bqk", [128, 2, 2], F32)
        w1_sb = sb("w1_sb", [128, 2, FF], F32)
        b1_sb = sb("b1_sb", [128, 4], F32)
        w2_sb = sb("w2_sb", [128, 4, D], F32)
        b2_sb = sb("b2_sb", [128, D], F32)
        wg_sb = sb("wg_sb", [128, 2, EX], F32)
        bg_sb = sb("bg_sb", [EX, 1], F32)
        eb_sb = sb("eb_sb", [128, 3, EX // 2], F32)
        gate_in = sb("gate_in", [128, 2], F32)
        gate = sb("gate", [128, 2], F32)
        eps = sb("eps", [128, 1], F32)
        ident = sb("ident", [128, 128], F32)
        spread = sb("spread", [128, 2, 128], F32)
        stats = sb("stats", [128, T // 128, 6], F32)
        moments = sb("moments", [128, T // 128, 2], F32)
        std = sb("std", [128, T // 128], F32)
        carrier = sb("carrier", [128, 1], F32)
        rstd = sb("rstd", [128, T // 128], F32)
        x2 = sb("x2", [128, QT, D], F32)
        xn2 = sb("xn2", [128, QT, D], F32)
        att_raw = sb("att_raw", [128, 2, QB], F32)
        den = sb("den", [128, QB], F32)
        rden = sb("rden", [128, QB], F32)
        pv_raw = sb("pv_raw", [128, 2, QB], F32)
        cmax = sb("cmax", [128, 2, HG * QT * 4], F32)
        negmax = sb("negmax", [128, 2, HG * QT], F32)
        neg_parts = sb("neg_parts", [HG * QT, 3, 128], BF16)
        neg_rest = sb("neg_rest", [HG * QT, 128], F32)
        split_g = sb("split_g", [128, 2, 7 * QB // 2], F32)

        def split_bufs(buf):
            return (buf[:, 0:QB], buf[:, QB:2 * QB],
                    buf[:, 2 * QB:2 * QB + 3 * QB // 2].bitcast(BF16).rearrange("p (j n) -> p j n", j=3))

        SPLIT = ([split_bufs(p_flat[:, i * 2 * QB * 2:(i * 2 + 2) * 2 * QB]) for i in range(2)],
                 [split_bufs(split_g[:, i, :]) for i in range(2)])

        q_scr = [dram(f"q_scr{m}", [6, 128, T], BF16) for m in range(2)]
        k_scr = [dram(f"k_scr{m}", [3, 128, S], BF16) for m in range(2)]
        xn2_scr = dram("xn2_scr", [T, D], F32)
        logit_scr = dram("logit_scr", [EX, T], F32)
        cand_scr = dram("cand_scr", [128, TOP], F32)
        cand_id_scr = dram("cand_id_scr", [128 * TOP, 1], U32)
        place_scr = dram("place_scr", [EX, TOP], U32)
        weight_scr = dram("weight_scr", [EX, TOP], F32)
        token_scr = dram("token_scr", [EX // 2, 128], U32)

        ps_s = pb("ps_s", [128, 4, 512], F32)
        ps_a = pb("ps_a", [128, 2, 512], F32)
        ps_v = pb("ps_v", [128, 512], F32)
        ps_m = pb("ps_m", [128, 512], F32)

        ctx_in, x_loaded, q_in, v_in, mlp_in = sem("ctx_in"), [sem(f"x_loaded{b}") for b in range(NB)], \
            sem("q_in"), sem("v_in"), sem("mlp_in")
        v_bias_rows = sem("v_bias_rows")
        gates_in, gates_ready = sem("gates_in"), sem("gates_ready")
        eps_ready, ident_zero, ident_ready, spread_zero, spread_ready = (
            sem("eps_ready"), sem("ident_zero"), sem("ident_ready"), sem("spread_zero"), sem("spread_ready"))
        ones_rows, v_ones, rden_zero = sem("ones_rows"), sem("v_ones"), sem("rden_zero")
        b2_scaled, x_biased = sem("b2_scaled"), sem("x_biased")
        ln_stat, ln_mean, ln_std, ln_rstd, ln_out = (
            sem("ln_stat"), sem("ln_mean"), sem("ln_std"), sem("ln_rstd"), sem("ln_out"))
        xt_filled, xt_free = sem("xt_filled"), sem("xt_free")
        proj_filled, proj_free, part1_ready = sem("proj_filled"), sem("proj_free"), sem("part1_ready")
        split_v, split_g_s = sem("split_v"), sem("split_g_s")
        stored = [sem(f"stored{c}") for c in range(NPROJ)]
        k_relaid = [sem(f"k_relaid{m}") for m in range(2)]
        q_loaded = [sem(f"q_loaded{g}") for g in range(NG)]
        a_filled, a_free, neg_ready = sem("a_filled"), sem("a_free"), sem("neg_ready")
        spare_filled, spare_free = sem("spare_filled"), sem("spare_free")
        neg_split, neg_rows = sem("neg_split"), sem("neg_rows")
        scores_ready, exp_done, pv_done, pv_out = (
            sem("scores_ready"), sem("exp_done"), sem("pv_done"), sem("pv_out"))
        att_moved, rden_ready = [sem(f"att_moved{i}") for i in range(2)], sem("rden_ready")
        x2_stored, xn2_stored, logit_stored = sem("x2_stored"), sem("xn2_stored"), sem("logit_stored")

        cand_space = sb("cand_space", [128, 1024], F32)
        chunk_logits = cand_space[:, 0:256]
        cand = cand_space[:, 256:256 + TOP]
        cand_pos = cand_space[:, 320:384].bitcast(U32)
        cand_id = cand_space[:, 384:448].bitcast(U32)
        cand_e = cand_space[0:EX, 448:448 + 8 * TOP]
        top_v = sb("top_v", [EX, TOP], F32)
        top_pos = sb("top_pos", [EX, TOP], U32)
        place_id = sb("place_id", [EX, TOP], U32)
        weight = sb("weight", [EX, TOP], F32)
        small = sb("small", [128, 8], F32)
        part_no = sb("part_no", [128, 1], I32)
        part_and = sb("part_and", [128, 1], I32)
        place_slot = sb("place_slot", [128, EX // 2], U32)
        weight_slot = sb("weight_slot", [128, EX // 2], F32)
        token_slot = sb("token_slot", [128, EX // 2], U32)
        token_exp = sb("token_exp", [TOP, EX], U32)
        tok_x = x_in[:, 0:EX // 2, :]
        h_in = xn_t[:, 0:8 * D].rearrange("p (a k n) -> p a k n", a=EX // 2, k=2)
        h_out = xn_t[:, 8 * D:16 * D].rearrange("p (a n) -> p a n", a=EX // 2)
        y_out = x_in[:, EX // 2:EX, :]
        w_in = [sem(f"w_in{l}") for l in range(3)]
        chunk_in, cand_ready, cand_stored, cand_id_stored, cand_e_in = (
            sem("chunk_in"), sem("cand_ready"), sem("cand_stored"), sem("cand_id_stored"), sem("cand_e_in"))
        offs_ready, top_step, place_ready, place_stored, place_in = (
            sem("offs_ready"), sem("top_step"), sem("place_ready"), sem("place_stored"), sem("place_in"))
        sum_ready, weight_ready, weight_stored, weight_in = (
            sem("sum_ready"), sem("weight_ready"), sem("weight_stored"), sem("weight_in"))
        negtop_ready, top_exp = sem("negtop_ready"), sem("top_exp")
        token_in = [sem(f"token_in{a}") for a in range(EX // 2)]
        token_stored, token_exp_in = sem("token_stored"), sem("token_exp_in")
        x_gathered = [sem(f"x_gathered{a}") for a in range(EX // 2)]
        t_filled, t_free, l_filled, l_free = sem("t_filled"), sem("t_free"), sem("l_filled"), sem("l_free")
        scattered = sem("scattered")
        chunk_off = small[:, 0:1]
        exp_off = small[0:EX, 1:2]
        neg_top = small[0:EX, 2:3]
        exp_sum = small[0:EX, 3:4]
        exp_rsum = small[0:EX, 4:5]
        ps_t = [ps_a[:, 0, :], ps_a[:, 1, :], ps_v[:, :], ps_m[:, :]]
        HALF = EX // 4

        block = es.enter_context(nc.Block())
        SPLITS_OF = lambda c: (0, c) if c < DVE_SPLITS else (1, c - DVE_SPLITS)

        NEG_DMAS, ATT_DMAS = 3 * 16, (HG + 1) * 16

        @block.sync
        def _(sp):
            for k in range(2):
                sp.dma_start(ctx_sb[0:CH, k, :], ctx_t[k * CH:(k + 1) * CH, :]).then_inc(ctx_in, 16)
            sp.dma_start(wk_sb[:, :, :], wk.rearrange("(k p) o -> p k o", k=2)).then_inc(ctx_in, 16)
            sp.dma_start(bqk[:, :, :], b_qk).then_inc(ctx_in, 16)
            for b in range(NB):
                sp.dma_start(x_in[:, b * QT:(b + 1) * QT, :],
                             x[b * QB:(b + 1) * QB, :].rearrange("(t p) d -> p t d", p=128)
                             ).then_inc(x_loaded[b], 16)
                if b == 0:
                    sp.dma_start(wq_sb[:, :, :], wq.rearrange("(k p) o -> p k o", k=2)).then_inc(q_in, 16)
                    sp.dma_start(gate_in[:, :], gates).then_inc(gates_in, 16)
            sp.dma_start(wv_sb[0:CH, :, :], wv.rearrange("(k p) o -> p k o", k=2)).then_inc(v_in, 16)
            sp.dma_start(wv_sb[CH:CH + 1, 1, :], bv).then_inc(v_in, 16)
            sp.dma_start(b2_sb[:, :], b2).then_inc(mlp_in, 16)
            sp.dma_start(w1_sb[:, :, :], w1.rearrange("(k p) o -> p k o", k=2)).then_inc(mlp_in, 16)
            sp.dma_start(b1_sb[:, :], b1).then_inc(mlp_in, 16)
            sp.dma_start(w2_sb[:, :, :], w2.rearrange("(k p) o -> p k o", k=4)).then_inc(mlp_in, 16)
            sp.dma_start(wg_sb[:, :, :], wg.rearrange("(k p) o -> p k o", k=2)).then_inc(mlp_in, 16)
            sp.dma_start(bg_sb[:, :], bg).then_inc(mlp_in, 16)
            sp.dma_start(eb_sb[:, :, :], eb).then_inc(mlp_in, 16)

            def store(c):
                kind, m, c0, n = PROJ[c]
                eng, i = SPLITS_OF(c)
                parts = SPLIT[eng][i % 2][2]
                sp.wait_ge((split_v, split_g_s)[eng], 3 * (i + 1))
                if kind == "k":
                    sp.dma_start(k_scr[m][:, :, c0:c0 + n].rearrange("j p n -> p j n"),
                                 parts[:, :, 0:n]).then_inc(stored[c], 16)
                else:
                    for j, (lo, hi) in enumerate(((0, 3), (3, 5), (5, 6))):
                        sp.dma_start(q_scr[m][lo:hi, :, c0:c0 + n].rearrange("j p n -> p j n"),
                                     parts[:, j:j + 1, 0:n].broadcast_to([128, hi - lo, n])
                                     ).then_inc(stored[c], 16)

            def relay_k(c):
                _, m, c0, n = PROJ[c]
                sp.wait_ge(stored[c], 16)
                for row, parts in ((0, 3), (3, 2), (5, 1)):
                    sp.dma_start(k_rows[row * DH:(row + parts) * DH, m * HM:(m + 1) * HM, c0:c0 + n],
                                 k_scr[m][0:parts, :, c0:c0 + n].rearrange("j (d h) n -> (j d) h n", h=HM)
                                 ).then_inc(k_relaid[m], 16)

            def load_q(s):
                m, h0 = s.g * HG // HM, s.g * HG % HM
                sp.dma_start(q_rows[0:PARTS, s.g, :, :],
                             q_scr[m].rearrange("j (d h) n -> (j d) h n", h=HM)
                             [:, h0:h0 + HG, bass.ds(s.block(scale=QB), QB)]).then_inc(q_loaded[s.g], 16)

            def put_neg(s):
                sp.wait_ge(neg_split, s.count(3, 3))
                for j in range(3):
                    sp.dma_start(q_rows[PARTS + j:PARTS + j + 1, s.g, :, :].rearrange("p h n -> p (h n)"),
                                 neg_parts[:, j, :]).then_inc(neg_rows, 16)

            def move_attention(s):
                wait(sp, pv_out, s.count(1, 1))
                if s.g == 0 and s.n0 >= NG:
                    wait(sp, spare_free, Step(s.n0 - NG, s.r).use("bc1") + 1)
                for h in range(HG):
                    r0 = (s.g % 2) * HG * DH + h * DH
                    sp.dma_start(att_raw[r0:r0 + DH, s.g // 2, :],
                                 pv_raw[32 * h:32 * h + DH, s.g % 2, :]).then_inc(att_moved[s.g % 2], 16)
                sp.dma_start(den[s.g * HG:(s.g + 1) * HG, :],
                             pv_raw[DH:128:32, s.g % 2, :]).then_inc(att_moved[s.g % 2], 16)

            def store_x2(b):
                wait(sp, spare_free, b.use("w2_3") + 1)
                sp.dma_start(out[bass.ds(b.block(scale=QB), QB), :].rearrange("(t p) d -> p t d", p=128),
                             x2[:, :, :]).then_inc(x2_stored, 16)

            def store_xn2(b):
                wait(sp, ln_out, b.block(1, QT) + NB * QT)
                sp.dma_start(xn2_scr[bass.ds(b.block(scale=QB), QB), :].rearrange("(t p) d -> p t d", p=128),
                             xn2[:, :, :]).then_inc(xn2_stored, 16)

            def store_logits(b):
                wait(sp, spare_free, b.use("lg") + 1)
                sp.dma_start(logit_scr[:, bass.ds(b.block(scale=QB), QB)],
                             logits[:, bass.ds(b.block(scale=QB), QB)]).then_inc(logit_stored, 16)

            first_second_half = next(c for c in range(NPROJ) if PROJ[c][:2] == ("q", 1))
            for c in range(first_second_half + 1):
                store(c)
                if c and PROJ[c - 1][0] == "k":
                    relay_k(c - 1)
                if PROJ[c][0] == "q":
                    sp.wait_ge(stored[c], 48)
                    if PROJ[c][1] == 0:
                        load_q(Step(0))
                        load_q(Step(1))
            for c in range(first_second_half + 1, NPROJ):
                store(c)
            put_neg(Step(0))

            def step(s):
                if s.n0 >= 1:
                    move_attention(s.after(-1))
                if s.n0 == 1:
                    for c in range(first_second_half + 1, NPROJ):
                        sp.wait_ge(stored[c], 48)
                prev = Step(s.n0 - NG, s.r)
                if s.n0 > NG and s.g == 1:
                    store_x2(prev)
                if s.n0 + 2 < STEPS:
                    wait(sp, scores_ready, s.count(PAIRS, -PAIRS))
                    load_q(s.after(2))
                if s.n0 > NG and s.g == 1:
                    store_xn2(prev)
                    store_logits(prev)
                if s.n0 + 1 < STEPS:
                    put_neg(s.after(1))

            run_steps(sp, step)
            last = Step(STEPS - 1)
            move_attention(last)

            sp.wait_ge(pv_done, KT * STEPS)
            for l in range(3):
                for k in range(2):
                    sp.dma_start(w_exp[:, l, :, k, :],
                                 ew[l][:, k * 128:(k + 1) * 128, :].rearrange("e p o -> p e o")
                                 ).then_inc(w_in[l], 16)
                if l == 0:
                    store_x2(last)
                    store_xn2(last)
                    store_logits(last)
            sp.wait_ge(logit_stored, 16 * NB)
            sp.dma_start(chunk_logits[:, :], logit_scr.rearrange("e (c n) -> (e c) n", c=8)
                         ).then_inc(chunk_in, 16)
            sp.wait_ge(cand_ready, 25)
            sp.dma_start(cand_scr, cand[:, :]).then_inc(cand_stored, 16)
            sp.dma_start(cand_id_scr.rearrange("(p n) o -> p (n o)", p=128), cand_id[:, :]
                         ).then_inc(cand_id_stored, 16)
            sp.wait_ge(cand_stored, 16)
            sp.dma_start(cand_e[:, :], cand_scr.rearrange("(e c) n -> e (c n)", e=EX)).then_inc(cand_e_in, 16)
            sp.wait_ge(place_ready, 1)
            sp.dma_start(place_scr, place_id[:, :]).then_inc(place_stored, 16)
            sp.wait_ge(place_stored, 16)
            sp.dma_start(place_slot[:, :], place_scr.rearrange("(a h) j -> (h j) a", h=2), allow_slow_non_contiguous=True
                         ).then_inc(place_in, 16)
            sp.wait_ge(weight_ready, 2)
            sp.dma_start(weight_scr, weight[:, :]).then_inc(weight_stored, 16)
            sp.wait_ge(weight_stored, 16)
            sp.dma_start(weight_slot[:, :], weight_scr.rearrange("(a h) j -> (h j) a", h=2), allow_slow_non_contiguous=True
                         ).then_inc(weight_in, 16)
            for a in range(EX // 2):
                sp.wait_ge(token_in[a], 16)
            sp.dma_start(token_scr.rearrange("a p -> p a"), token_slot[:, :], allow_slow_non_contiguous=True).then_inc(token_stored, 16)
            sp.wait_ge(token_stored, 16)
            sp.dma_start(token_exp[:, :], token_scr.rearrange("a (h j) -> j (a h)", h=2), allow_slow_non_contiguous=True
                         ).then_inc(token_exp_in, 16)


        @block.gpsimd
        def _(pool):
            pool.memset(ident[:, :], 0.0).then_inc(ident_zero, 1)
            pool.wait_ge(ident_zero, 1)
            pool.affine_select(out=ident[:, :], in_=ident[:, :], compare_op=ALU.not_equal, fill=1.0, base=0,
                               pattern=[[-1, 128]], channel_multiplier=1).then_inc(ident_ready, 1)
            pool.wait_ge(ident_ready, 1)
            pool.memset(k_rows[PARTS:PARTS + 3, :, :], 1.0).then_inc(ones_rows, 1)
            pool.wait_ge(ones_rows, 1)
            pool.memset(ctx_sb[CH:CH + 1, 1, :], 1.0).then_inc(v_bias_rows, 1)
            pool.wait_ge(v_bias_rows, 1)
            pool.memset(v_cols[:, :, :, :], 1.0).then_inc(v_ones, 1)
            pool.memset(spread[:, :, :], 0.0).then_inc(spread_zero, 1)
            pool.wait_ge(spread_zero, 1)
            pool.affine_select(out=spread[:, :, :].rearrange("p k (h d) -> p k h d", d=DH),
                               in_=spread[:, :, :].rearrange("p k (h d) -> p k h d", d=DH),
                               compare_op=ALU.not_equal, fill=1.0, base=0,
                               pattern=[[-HM, 2], [-1, HM], [0, DH]], channel_multiplier=1
                               ).then_inc(spread_ready, 1)
            pool.memset(rden[:, :], 0.0).then_inc(rden_zero, 1)

            def split(c):
                kind, m, c0, n = PROJ[c]
                i = c - DVE_SPLITS
                full, rest, parts = SPLIT[1][i % 2]
                pool.wait_ge(part1_ready, c + 1)
                pool.tensor_tensor(out=rest[:, 0:n], in0=full[:, 0:n], in1=parts[:, 0, 0:n],
                                   op=ALU.subtract).then_inc(split_g_s, 1)
                pool.wait_ge(split_g_s, 3 * i + 1)
                pool.tensor_copy(parts[:, 1, 0:n], rest[:, 0:n]).then_inc(split_g_s, 1)
                pool.wait_ge(split_g_s, 3 * i + 2)
                pool.tensor_tensor(out=parts[:, 2, 0:n], in0=rest[:, 0:n], in1=parts[:, 1, 0:n],
                                   op=ALU.subtract).then_inc(split_g_s, 1)

            for c in range(DVE_SPLITS, NPROJ):
                split(c)
            pool.wait_ge(b2_scaled, 1)
            for t in range(T // 128):
                if t == 0:
                    pool.wait_ge(ln_out, T // 128)
                pool.tensor_tensor(out=x_in[:, t, :], in0=x_in[:, t, :], in1=b2_sb[:, :],
                                   op=ALU.add).then_inc(x_biased, 1)
            pool.iota(part_no[:, :], [[0, 1]], base=0, channel_multiplier=1).then_inc(offs_ready, 1)

            pool.wait_ge(place_in, 16)
            pool.wait_ge(cand_id_stored, 16)
            for a in range(EX // 2):
                pool.indirect_dma_start(token_slot[:, a:a + 1], None, cand_id_scr,
                                        bass.IndirectOffsetOnAxis(place_slot[:, a:a + 1], 0),
                                        bounds_check=128 * TOP - 1).then_inc(token_in[a], 16)
            pool.wait_ge(xn2_stored, 16 * NB)
            pool.wait_ge(spare_free, ORDER[("w2_3", NB - 1)] + 1)
            for a in range(EX // 2):
                pool.wait_ge(token_in[a], 16)
                pool.indirect_dma_start(tok_x[:, a, :], None, xn2_scr,
                                        bass.IndirectOffsetOnAxis(token_slot[:, a:a + 1], 0),
                                        bounds_check=T - 1).then_inc(x_gathered[a], 16)
            pool.wait_ge(token_exp_in, 16)
            pool.wait_ge(x2_stored, 16 * NB)
            for e in range(EX):
                a = e // 2
                g, a4 = a // HALF, a % HALF
                pool.wait_ge(l_free, (g * 3 + 2) * HALF + a4 + 1)
                if e:
                    pool.wait_ge(scattered, 16 * e)
                r0 = (e % 2) * TOP
                pool.indirect_dma_start(out, bass.IndirectOffsetOnAxis(token_exp[:, e:e + 1], 0),
                                        y_out[r0:r0 + TOP, a, :], None, compute_op=ALU.add,
                                        bounds_check=T - 1).then_inc(scattered, 16)
            pool.wait_ge(scattered, 16 * EX)

        @block.scalar
        def _(act):
            act.wait_ge(gates_in, 16)
            act.activation(gate[:, :], gate_in[:, :], ACT.Tanh).then_inc(gates_ready, 1)
            act.wait_ge(eps_ready, 1)

            def block_std(b):
                act.wait_ge(ln_mean, QT * (b + 1))
                tiles = slice(b * QT, (b + 1) * QT)
                act.activation(std[:, tiles], moments[:, tiles, 1], ACT.Sqrt, bias=eps[:, :]).then_inc(ln_std, 1)

            def transposed_x(b):
                for k in range(2):
                    act.wait_ge(xt_filled, 2 * b + k + 1)
                    act.activation(xn_tv[:, k, b * QB:(b + 1) * QB], (ps_m if k == 0 else ps_v)[:, :],
                                   ACT.Copy).then_inc(xt_free, 1)

            def projected(c):
                kind, m, c0, n = PROJ[c]
                eng, i = SPLITS_OF(c)
                full, _, parts = SPLIT[eng][i % 2]
                act.wait_ge(proj_filled, c + 1)
                if i >= 2:
                    act.wait_ge(stored[c - 2], 16 * STORES[PROJ[c - 2][0]])
                act.activation(full[:, 0:n], ps_s[:, c % 4, 0:n], ACT.Identity,
                               bias=bqk[:, 0 if kind == "q" else 1, m:m + 1]).then_inc(proj_free, 1)
                act.wait_ge(proj_free, c + 1)
                act.activation(parts[:, 0, 0:n], full[:, 0:n], ACT.Copy).then_inc(part1_ready, 1)

            def values(v):
                keys = 128 if v < KT - 1 else KLAST
                act.wait_ge(proj_filled, NPROJ + v + 1)
                if v == 0:
                    act.wait_ge(v_ones, 1)
                act.activation(v_cols[0:keys, v, :, 0:DH],
                               ps_s[0:keys, (NPROJ + v) % 4, 0:D].rearrange("p (h d) -> p h d", h=H),
                               ACT.Copy).then_inc(proj_free, 1)

            act.wait_ge(ctx_in, 64)
            for c in range(4):
                projected(c)
            block_std(0)
            transposed_x(0)
            for what, i in PROLOGUE[5:]:
                if what == "proj":
                    projected(i)
                    if i == 8:
                        for b in range(1, NB):
                            block_std(b)
                elif what == "xt":
                    transposed_x(i)
                elif what == "v":
                    values(i)

            act.wait_ge(mlp_in, 16 * 7)

            def unit(s, name):
                b = Step(s.n0 - NG, s.r)
                if name.startswith("w1_"):
                    m = int(name[3])
                    wait(act, spare_filled, b.use(name) + 1)
                    act.activation(hidden[:, m, :], ps_m[:, :], ACT.Relu,
                                   bias=b1_sb[:, m:m + 1]).then_inc(spare_free, 1)
                elif name.startswith("tr"):
                    wait(act, spare_filled, b.use(name) + 1)
                    act.activation(xn2_t[:, int(name[2]), :], ps_m[:, :], ACT.Copy).then_inc(spare_free, 1)
                elif name == "lg":
                    wait(act, spare_filled, b.use(name) + 1)
                    act.activation(logits[:, bass.ds(b.block(scale=QB), QB)], ps_m[0:EX, :], ACT.Identity,
                                   bias=bg_sb[:, :]).then_inc(spare_free, 1)

            def router_std(b):
                wait(act, ln_mean, b.block(1, QT) + NB * QT)
                act.activation(std[:, 0:QT], moments[:, 0:QT, 1], ACT.Sqrt, bias=eps[:, :]).then_inc(ln_std, 1)

            def pv_copy(s):
                wait(act, pv_done, s.count(KT, KT))
                if s.n0 >= 2:
                    wait(act, att_moved[s.g % 2], s.halves(ATT_DMAS))
                act.activation(pv_raw[:, s.g % 2, :], ps_v[:, :], ACT.Copy).then_inc(pv_out, 1)

            def step(s):
                units = dict()
                for kt, name in plan(s.n0):
                    units.setdefault(kt, []).append(name)
                for kt in range(KT):
                    keys = 128 if kt < KT - 1 else KLAST
                    for hp in range(2):
                        j = 2 * kt + hp
                        wait(act, scores_ready, s.count(PAIRS, j + 1))
                        if hp == 0 and s.n0 * KT + kt >= 2:
                            wait(act, pv_done, s.count(KT, kt - 1))
                        slot = (s.g * PAIRS + j) % 4
                        act.activation(probs[0:keys, slot, :, :], ps_s[0:keys, 2 * hp:2 * hp + 2, :], ACT.Exp,
                                       scale=SCALE).then_inc(exp_done, 1)
                    if kt == 0 and s.n0 >= 1:
                        pv_copy(s.after(-1))
                    if kt == 1 and s.n0 > NG and s.g == 1:
                        router_std(Step(s.n0 - NG, s.r))
                    for name in units.get(kt, []):
                        unit(s, name)

            run_steps(act, step)
            last = Step(STEPS - 1)
            pv_copy(last)
            past = Step(STEPS)
            for _, name in MLP_UNITS:
                unit(past, name)
            router_std(last)
            for _, name in LN_UNITS:
                unit(past, name)

            act.wait_ge(negtop_ready, 1)
            act.wait_ge(spare_free, len(ORDER))
            act.activation(xn_t[0:EX, 0:T], logits[:, :], ACT.Exp, bias=neg_top,
                           accum_out=exp_sum).then_inc(sum_ready, 1)
            act.wait_ge(place_ready, 1)
            act.activation(weight[:, :], top_v[:, :], ACT.Exp, bias=neg_top).then_inc(top_exp, 1)
            for g in range(2):
                for l in range(2):
                    for a4 in range(HALF):
                        a = g * HALF + a4
                        q = (g * 3 + l) * HALF + a4
                        act.wait_ge(l_filled, q + 1)
                        act.activation(h_out[:, a, :], ps_s[:, a4, 0:D], ACT.Relu,
                                       bias=eb_sb[:, l, a:a + 1]).then_inc(l_free, 1)
                for a4 in range(HALF):
                    q = (g * 3 + 2) * HALF + a4
                    act.wait_ge(l_free, q + 1)

        @block.vector
        def _(dve):
            dve.memset(eps[:, :], EPS).then_inc(eps_ready, 1)

            def moments_of(src, base, t0=0):
                for t in range(QT):
                    dve.bn_stats(stats[:, t0 + t, :], src[:, t, :]).then_inc(ln_stat, 1)
                wait(dve, ln_stat, base + QT)
                if not isinstance(base, int):
                    dve.memset(carrier[:, :], 0.0)
                for t in range(QT):
                    dve.bn_aggr(moments[:, t0 + t, :], stats[:, t0 + t, :]).then_inc(ln_mean, 1)

            def normalise(src, blocks_before, t0=0):
                wait(dve, ln_std, blocks_before + 1)
                dve.reciprocal(rstd[:, t0:t0 + QT], std[:, t0:t0 + QT]).then_inc(ln_rstd, 1)
                wait(dve, ln_rstd, blocks_before + 1)
                for t in range(QT):
                    dve.tensor_scalar(xn2[:, t, :], src[:, t, :], moments[:, t0 + t, 0:1], rstd[:, t0 + t:t0 + t + 1],
                                      ALU.subtract, ALU.mult).then_inc(ln_out, 1)

            def split(c):
                kind, m, c0, n = PROJ[c]
                full, rest, parts = SPLIT[0][c % 2]
                dve.wait_ge(part1_ready, c + 1)
                dve.tensor_tensor(out=rest[:, 0:n], in0=full[:, 0:n], in1=parts[:, 0, 0:n],
                                  op=ALU.subtract).then_inc(split_v, 1)
                dve.wait_ge(split_v, 3 * c + 1)
                dve.tensor_copy(parts[:, 1, 0:n], rest[:, 0:n]).then_inc(split_v, 1)
                dve.wait_ge(split_v, 3 * c + 2)
                dve.tensor_tensor(out=parts[:, 2, 0:n], in0=rest[:, 0:n], in1=parts[:, 1, 0:n],
                                  op=ALU.subtract).then_inc(split_v, 1)

            def x_moments(b):
                dve.wait_ge(x_loaded[b], 16)
                moments_of(x_in[:, b * QT:(b + 1) * QT, :], QT * b, QT * b)

            def x_normal(b):
                if b:
                    dve.wait_ge(xt_filled, 2 * b)
                dve.wait_ge(ln_mean, QT * (b + 1))
                normalise(x_in[:, b * QT:(b + 1) * QT, :], b, QT * b)

            for c in range(4):
                split(c)
            x_moments(0)
            x_normal(0)
            split(4)
            for b in range(1, NB):
                x_moments(b)
            dve.wait_ge(mlp_in, 16 * 7)
            dve.wait_ge(gates_ready, 1)
            dve.tensor_scalar(b2_sb[:, :], b2_sb[:, :], gate[:, 0:1], None, ALU.mult).then_inc(b2_scaled, 1)

            def row_max(s, t, h, c):
                g_local = (t * HG + h) * 4 + c
                if g_local == 0 and s.n0 >= 2:
                    wait(dve, neg_ready, s.count(1, -1))
                wait(dve, a_filled, s.count(ACH, g_local + 1))
                col = (h * QT + t) * 4 + c
                dve.reduce_max(cmax[:, s.g % 2, col:col + 1], ps_a[:, g_local % 2, 0:CHUNKS[c][1]],
                               AX.X).then_inc(a_free, 1)

            def neg_max(s):
                wait(dve, a_free, s.count(ACH, ACH))
                if s.n0 >= 2:
                    wait(dve, spare_filled, Step(s.n0 - 2, s.r).use("neg") + 1)
                dve.tensor_reduce(out=negmax[:, s.g % 2, :],
                                  in_=cmax[:, s.g % 2, :].rearrange("p (u c) -> p u c", c=4),
                                  axis=AX.X, op=ALU.max, negate=True).then_inc(neg_ready, 1)

            def neg_to_parts(s):
                wait(dve, spare_filled, s.use("neg") + 1)
                if s.n0 >= 1:
                    wait(dve, neg_rows, s.count(NEG_DMAS))
                dve.tensor_copy(neg_parts[:, 0, :], ps_m[0:HG * QT, 0:128]).then_inc(neg_split, 1)
                wait(dve, neg_split, s.count(3, 1))
                dve.tensor_tensor(out=neg_rest[:, :], in0=ps_m[0:HG * QT, 0:128], in1=neg_parts[:, 0, :],
                                  op=ALU.subtract).then_inc(spare_free, 1)
                wait(dve, spare_free, s.use("neg") + 1)
                dve.tensor_copy(neg_parts[:, 1, :], neg_rest[:, :]).then_inc(neg_split, 1)
                wait(dve, neg_split, s.count(3, 2))
                dve.tensor_tensor(out=neg_parts[:, 2, :], in0=neg_rest[:, :], in1=neg_parts[:, 1, :],
                                  op=ALU.subtract).then_inc(neg_split, 1)

            def unit(s, name):
                b = Step(s.n0 - NG, s.r)
                if name == "neg":
                    neg_to_parts(s.after(1))
                elif name.startswith("bc"):
                    k = int(name[2])
                    wait(dve, spare_filled, b.use(name) + 1)
                    dve.tensor_tensor(out=att_t[:, k, :], in0=ps_m[:, :], in1=att_raw[:, k, :],
                                      op=ALU.mult).then_inc(spare_free, 1)
                elif name.startswith("w2_"):
                    t = int(name[3])
                    if t == 0 and s.n0 >= 2 * NG:
                        wait(dve, x2_stored, b.block(scale=16))
                    wait(dve, spare_filled, b.use(name) + 1)
                    if t == 0 and s.n0 == NG and s.r is None or t == 0:
                        dve.wait_ge(x_biased, T // 128)
                    dve.scalar_tensor_tensor(out=x2[:, t, :], in0=ps_m[:, 0:D], scalar=gate[:, 0:1],
                                             in1=x_in[:, bass.ds(b.block(scale=QT) + t, 1), :]
                                             .rearrange("p o d -> p (o d)"),
                                             op0=ALU.mult, op1=ALU.add).then_inc(spare_free, 1)

            def denominators(b):
                for parity in range(2):
                    wait(dve, att_moved[parity], b.block(1, NG // 2 * ATT_DMAS))
                dve.wait_ge(rden_zero, 1)
                dve.reciprocal(rden[0:H, :], den[0:H, :]).then_inc(rden_ready, 1)

            def router_moments(b):
                wait(dve, spare_free, b.use("w2_3") + 1)
                wait(dve, ln_out, b.block(0, QT) + NB * QT)
                wait(dve, ln_mean, b.block(0, QT) + NB * QT)
                moments_of(x2[:, :, :], b.block(0, QT) + NB * QT)

            def router_norm(b, first):
                if not first:
                    wait(dve, xn2_stored, b.block(scale=16))
                wait(dve, ln_mean, b.block(1, QT) + NB * QT)
                normalise(x2[:, :, :], b.block() + NB)

            def between(s, kt, done):
                prev = Step(s.n0 - NG, s.r)
                if s.n0 >= NG and s.g == 0 and kt == 2:
                    denominators(prev)
                if s.n0 > NG and s.g == 1 and kt == 0:
                    router_moments(prev)
                if s.n0 > NG and s.g == 1 and kt == 2:
                    router_norm(prev, False)
                for at, name in plan(s.n0):
                    if at == kt:
                        unit(s, name)

            def step(s):
                chunks = row_max_chunks(s.n0)
                for kt in range(KT):
                    for i in range(5 * kt, min(5 * kt + 5, len(chunks))):
                        if i == 5 * kt + 4:
                            between(s, kt, i)
                        ahead, t, h, c = chunks[i]
                        row_max(s.after(ahead), t, h, c)
                        if (t, h, c) == (QT - 1, HG - 1, 3):
                            neg_max(s.after(ahead))
                    if 5 * kt + 4 >= len(chunks):
                        between(s, kt, len(chunks))

            for what, i in PROLOGUE_DVE:
                if what == "xt":
                    x_normal(i)
                else:
                    q, h = i
                    for c in range(4):
                        row_max(Step(q // QT), q % QT, h, c)
                    if i == (QT - 1, HG - 1):
                        neg_max(Step(0))
            neg_to_parts(Step(0))
            run_steps(dve, step)

            last, past = Step(STEPS - 1), Step(STEPS)
            denominators(last)
            for _, name in MLP_UNITS:
                unit(past, name)
            router_moments(last)
            router_norm(last, False)

            dve.wait_ge(offs_ready, 1)
            dve.tensor_scalar(part_and[:, :], part_no[:, :], 7, None, ALU.bitwise_and).then_inc(offs_ready, 1)
            dve.wait_ge(offs_ready, 2)
            dve.tensor_scalar(chunk_off, part_and[:, :], 256.0, None, ALU.mult).then_inc(offs_ready, 1)
            dve.tensor_scalar(exp_off, part_no[0:EX, :], float(8 * TOP), None, ALU.mult).then_inc(offs_ready, 1)
            dve.wait_ge(chunk_in, 16)
            n = 0
            for k in range(TOP // 8):
                top8 = cand[:, 8 * k:8 * k + 8]
                if n:
                    dve.wait_ge(cand_ready, n)
                dve.max(top8, chunk_logits).then_inc(cand_ready, 1)
                dve.wait_ge(cand_ready, n + 1)
                dve.max_index(cand_pos[:, 8 * k:8 * k + 8], top8, chunk_logits).then_inc(cand_ready, 1)
                dve.wait_ge(cand_ready, n + 2)
                dve.match_replace(chunk_logits, top8, chunk_logits, -3e38).then_inc(cand_ready, 1)
                n += 3
            dve.wait_ge(cand_ready, n)
            dve.wait_ge(offs_ready, 4)
            dve.tensor_scalar(cand_id, cand_pos, chunk_off, None, ALU.add).then_inc(cand_ready, 1)
            dve.wait_ge(cand_e_in, 16)
            n = 0
            for k in range(TOP // 8):
                top8 = top_v[:, 8 * k:8 * k + 8]
                if n:
                    dve.wait_ge(top_step, n)
                dve.max(top8, cand_e).then_inc(top_step, 1)
                dve.wait_ge(top_step, n + 1)
                if k == 0:
                    dve.tensor_scalar(neg_top, top_v[:, 0:1], -1.0, None, ALU.mult).then_inc(negtop_ready, 1)
                dve.max_index(top_pos[:, 8 * k:8 * k + 8], top8, cand_e).then_inc(top_step, 1)
                dve.wait_ge(top_step, n + 2)
                dve.match_replace(cand_e, top8, cand_e, -3e38).then_inc(top_step, 1)
                n += 3
            dve.wait_ge(top_step, n)
            dve.tensor_scalar(place_id[:, :], top_pos[:, :], exp_off, None, ALU.add).then_inc(place_ready, 1)
            dve.wait_ge(sum_ready, 1)
            dve.reciprocal(exp_rsum, exp_sum).then_inc(weight_ready, 1)
            dve.wait_ge(weight_ready, 1)
            dve.wait_ge(top_exp, 1)
            dve.tensor_scalar(weight[:, :], weight[:, :], exp_rsum, gate[0:EX, 1:2], ALU.mult, ALU.mult
                              ).then_inc(weight_ready, 1)
            for g in range(2):
                for l in range(3):
                    for a4 in range(HALF):
                        a = g * HALF + a4
                        q = (g * 3 + l) * HALF + a4
                        dve.wait_ge(t_filled, q + 1)
                        if q == 0:
                            dve.wait_ge(sum_ready, 1)
                        dve.tensor_copy(h_in[:, a, :, :], ps_t[a4][:, 0:2 * 128]
                                        .rearrange("p (k n) -> p k n", k=2)).then_inc(t_free, 1)
                for a4 in range(HALF):
                    a = g * HALF + a4
                    q = (g * 3 + 2) * HALF + a4
                    dve.wait_ge(l_filled, q + 1)
                    if q == 2 * HALF:
                        dve.wait_ge(weight_in, 16)
                    dve.tensor_scalar(y_out[:, a, :], ps_s[:, a4, 0:D], eb_sb[:, 2, a:a + 1],
                                      weight_slot[:, a:a + 1], ALU.add, ALU.mult).then_inc(l_free, 1)

        @block.tensor
        def _(pe):
            def project(c):
                kind, m, c0, n = PROJ[c]
                if c >= 4:
                    pe.wait_ge(proj_free, c - 3)
                w, src = (wk_sb, ctx_sb) if kind == "k" else (wq_sb, xn_tv)
                rows = CH if kind == "k" else 128
                if kind == "q":
                    pe.wait_ge(xt_free, 2 * (c0 // QB) + 2)
                for k in range(2):
                    last = pe.matmul(ps_s[:, c % 4, 0:n], w[0:rows, k, m * 128:(m + 1) * 128],
                                     src[0:rows, k, c0:c0 + n], start=k == 0, stop=k == 1)
                last.then_inc(proj_filled, 1)

            def transpose_x(b):
                pe.wait_ge(ln_out, QT * (b + 1))
                for k in range(2):
                    if b:
                        pe.wait_ge(xt_free, 2 * b + k - 1)
                    for t in range(QT):
                        last = pe.transpose((ps_m if k == 0 else ps_v)[:, t * 128:(t + 1) * 128],
                                            xn2[:, t, k * 128:(k + 1) * 128], ident[:, :])
                    last.then_inc(xt_filled, 1)

            def values(v):
                keys = 128 if v < KT - 1 else KLAST
                pe.wait_ge(proj_free, NPROJ + v - 3)
                for k in range(2):
                    rows = CH + k
                    last = pe.matmul(ps_s[0:keys, (NPROJ + v) % 4, 0:D], ctx_sb[0:rows, k, v * 128:v * 128 + keys],
                                     wv_sb[0:rows, k, :], start=k == 0, stop=k == 1)
                last.then_inc(proj_filled, 1)

            def row_max(s, t, h, c):
                g_local = (t * HG + h) * 4 + c
                if g_local == 0:
                    wait(pe, q_loaded[s.g], s.block(1, 16))
                    if s.n0 == 0:
                        pe.wait_ge(k_relaid[0], 12 * 16)
                    if s.n0 == HM // HG:
                        pe.wait_ge(k_relaid[1], 12 * 16)
                if s.n0 or g_local >= 2:
                    wait(pe, a_free, s.count(ACH, g_local - 1))
                c0, n = CHUNKS[c]
                head = s.g * HG + h
                pe.matmul(ps_a[:, g_local % 2, 0:n], q_rows[0:PARTS, s.g, h, t * 128:(t + 1) * 128],
                          k_rows[0:PARTS, head, c0:c0 + n], start=True, stop=True).then_inc(a_filled, 1)

            def transpose_neg(s):
                wait(pe, neg_ready, s.count(1, 1))
                if s.n0:
                    wait(pe, spare_free, s.use("neg"))
                else:
                    pe.wait_ge(xt_free, 2 * NB)
                pe.transpose(ps_m[0:HG * QT, 0:128], negmax[:, s.g % 2, :], ident[:, :]).then_inc(spare_filled, 1)

            def unit(s, name):
                b = Step(s.n0 - NG, s.r)
                if name == "neg":
                    return transpose_neg(s.after(1))
                wait(pe, spare_free, b.use(name))
                if name.startswith("bc"):
                    if name == "bc0":
                        wait(pe, rden_ready, b.block(1))
                    last = pe.matmul(ps_m[:, :], spread[:, int(name[2]), :], rden[:, :], start=True, stop=True)
                elif name.startswith("w1_"):
                    m = int(name[3])
                    for k in range(2):
                        last = pe.matmul(ps_m[:, :], w1_sb[:, k, m * 128:(m + 1) * 128], att_t[:, k, :],
                                         start=k == 0, stop=k == 1)
                elif name.startswith("w2_"):
                    t = int(name[3])
                    for k in range(4):
                        last = pe.matmul(ps_m[:, 0:D], hidden[:, k, t * 128:(t + 1) * 128], w2_sb[:, k, :],
                                         start=k == 0, stop=k == 3)
                elif name.startswith("tr"):
                    k = int(name[2])
                    wait(pe, ln_out, b.block(1, QT) + NB * QT)
                    for t in range(QT):
                        last = pe.transpose(ps_m[:, t * 128:(t + 1) * 128], xn2[:, t, k * 128:(k + 1) * 128],
                                            ident[:, :])
                elif name == "lg":
                    for k in range(2):
                        last = pe.matmul(ps_m[0:EX, :], wg_sb[:, k, :], xn2_t[:, k, :], start=k == 0, stop=k == 1)
                last.then_inc(spare_filled, 1)

            def times_v(s, kt):
                keys = 128 if kt < KT - 1 else KLAST
                wait(pe, exp_done, s.count(PAIRS, 2 * kt + 2))
                if kt == 0 and s.n0:
                    wait(pe, pv_out, s.count(1))
                for h in range(HG):
                    slot = (s.g * PAIRS + 2 * kt + h // 2) % 4
                    last = pe.matmul(ps_v[32 * h:32 * h + DH + 1, :], v_cols[0:keys, kt, s.g * HG + h, :],
                                     probs[0:keys, slot, h % 2, :], start=kt == 0, stop=kt == KT - 1)
                last.then_inc(pv_done, 1)

            def step(s):
                chunks = row_max_chunks(s.n0)
                todo = iter(chunks)

                def next_chunk():
                    for ahead, t, h, c in todo:
                        row_max(s.after(ahead), t, h, c)
                        break

                for kt in range(KT):
                    keys = 128 if kt < KT - 1 else KLAST
                    for h in range(HG):
                        j = 2 * kt + h // 2
                        if h % 2 == 0 and s.n0 * PAIRS + j >= 2:
                            wait(pe, exp_done, s.count(PAIRS, j - 1))
                        if kt == 0 and h == 0:
                            wait(pe, neg_rows, s.count(NEG_DMAS, NEG_DMAS))
                        mm = pe.matmul(ps_s[0:keys, h, :], k_rows[0:PARTS + 3, s.g * HG + h, kt * 128:kt * 128 + keys],
                                       q_rows[0:PARTS + 3, s.g, h, :], start=True, stop=True)
                        if h % 2:
                            mm.then_inc(scores_ready, 1)
                        next_chunk()
                    if kt:
                        times_v(s, kt - 1)
                    elif s.n0:
                        times_v(s.after(-1), KT - 1)
                    for at, name in plan(s.n0):
                        if at == kt:
                            unit(s, name)
                    next_chunk()

            pe.wait_ge(ctx_in, 64)
            pe.wait_ge(ident_ready, 1)
            for what, i in PROLOGUE:
                if what == "proj":
                    if PROJ[i][0] == "q":
                        pe.wait_ge(q_in, 16)
                    project(i)
                elif what == "xt":
                    transpose_x(i)
                elif what == "v":
                    if i == 0:
                        pe.wait_ge(v_in, 32)
                        pe.wait_ge(v_bias_rows, 1)
                    values(i)
                else:
                    q, h = i
                    for c in range(4):
                        row_max(Step(q // QT), q % QT, h, c)
            transpose_neg(Step(0))
            pe.wait_ge(proj_free, NPROJ + KT)
            pe.wait_ge(ones_rows, 1)
            pe.wait_ge(mlp_in, 16 * 7)
            pe.wait_ge(spread_ready, 1)
            run_steps(pe, step)

            last, past = Step(STEPS - 1), Step(STEPS)
            times_v(last, KT - 1)
            for _, name in MLP_UNITS + LN_UNITS:
                unit(past, name)

            pe.wait_ge(spare_free, len(ORDER))
            for g in range(2):
                for l in range(3):
                    for a4 in range(HALF):
                        a = g * HALF + a4
                        q = (g * 3 + l) * HALF + a4
                        if l == 0:
                            pe.wait_ge(x_gathered[a], 16)
                            src = tok_x[:, a, :]
                            if q >= HALF:
                                pe.wait_ge(t_free, q - HALF + 1)
                        else:
                            pe.wait_ge(l_free, q - HALF + 1)
                            src = h_out[:, a, :]
                        for k in range(2):
                            last = pe.transpose(ps_t[a4][:, k * 128:(k + 1) * 128],
                                                src[:, k * 128:(k + 1) * 128], ident[:, :])
                        last.then_inc(t_filled, 1)
                    for a4 in range(HALF):
                        a = g * HALF + a4
                        q = (g * 3 + l) * HALF + a4
                        if a4 == 0 and g == 0:
                            pe.wait_ge(w_in[l], 32)
                        pe.wait_ge(t_free, q + 1)
                        if q >= HALF:
                            pe.wait_ge(l_free, q - HALF + 1)
                        for k in range(2):
                            for e2 in range(2):
                                last = pe.matmul(ps_s[e2 * TOP:(e2 + 1) * TOP, a4, 0:D],
                                                 h_in[:, a, k, e2 * TOP:(e2 + 1) * TOP],
                                                 w_exp[:, l, 2 * a + e2, k, :], start=k == 0, stop=k == 1)
                        last.then_inc(l_filled, 1)


def prologue_order():
    order = [("proj", c) for c in range(4)] + [("xt", 0), ("proj", 4)] + [("proj", c) for c in range(5, 9)]
    rest = [("proj", 9), ("xt", 1), ("proj", 10), ("proj", 11), ("xt", 2), ("proj", 12), ("proj", 13),
            ("xt", 3), ("proj", 14), ("proj", 15)] + [("v", v) for v in range(KT)]
    for q in range(QT + LEAD):
        for h in range(HG):
            order.append(("max", (q, h)))
            order += rest[:2] if len(rest) > 4 * (QT + LEAD) - (q * HG + h) else rest[:1]
            rest = rest[2:] if len(rest) > 4 * (QT + LEAD) - (q * HG + h) else rest[1:]
    return order + rest


def prologue_order_dve():
    order = [u for u in PROLOGUE if u[0] == "max" or u[0] == "xt" and u[1]]
    for b in range(1, NB):
        at = order.index(("xt", b))
        order[at - 1:at + 1] = [order[at], order[at - 1]]
    return order


PROLOGUE = prologue_order()
PROLOGUE_DVE = prologue_order_dve()


def kernel(x, ctx_768, g_xattn, g_ffn, L0_xattn_Wq, L0_xattn_bq, L0_xattn_Wk, L0_xattn_bk, L0_xattn_Wv,
           L0_xattn_bv, L0_xattn_W1, L0_xattn_b1, L0_xattn_W2, L0_xattn_b2, L0_ffn_Wg, L0_ffn_bg, L0_ffn_w1,
           L0_ffn_b1, L0_ffn_w2, L0_ffn_b2, L0_ffn_w3, L0_ffn_b3):
    import numpy as np
    import concourse.bacc as bacc
    from concourse.bass_utils import run_bass_kernel_spmd

    def d_major(a):
        a = np.asarray(a)
        return a.reshape(-1, 2, HM, DH).transpose(0, 1, 3, 2).reshape(-1, D)

    def rows(a, k):
        return np.asarray(a).reshape(k, 128).T

    arrays = {
        "x": np.asarray(x)[0],
        "ctx_t": np.asarray(ctx_768)[0].T,
        "wq": d_major(L0_xattn_Wq),
        "bqk": np.stack([rows(d_major(L0_xattn_bq), 2), rows(d_major(L0_xattn_bk), 2)], axis=1),
        "wk": d_major(L0_xattn_Wk),
        "wv": np.asarray(L0_xattn_Wv),
        "bv": np.asarray(L0_xattn_bv).reshape(1, D),
        "w1": np.asarray(L0_xattn_W1),
        "b1": rows(L0_xattn_b1, 4),
        "w2": np.asarray(L0_xattn_W2),
        "b2": np.broadcast_to(np.asarray(L0_xattn_b2), (128, D)),
        "wg": np.asarray(L0_ffn_Wg),
        "bg": np.asarray(L0_ffn_bg).reshape(EX, 1),
        "gates": np.broadcast_to(np.concatenate([np.asarray(g_xattn), np.asarray(g_ffn)]), (128, 2)),
        "ew1": np.asarray(L0_ffn_w1),
        "ew2": np.asarray(L0_ffn_w2),
        "ew3": np.asarray(L0_ffn_w3),
        "eb": np.stack([np.repeat(np.asarray(b).reshape(EX // 2, 2).T, TOP, axis=0)
                        for b in (L0_ffn_b1, L0_ffn_b2, L0_ffn_b3)], axis=1),
    }
    arrays = {k: np.ascontiguousarray(v) for k, v in arrays.items()}
    nc = bacc.Bacc("TRN2", target_bir_lowering=False, num_devices=1)
    ap = {k: nc.dram_tensor("in_" + k, v.shape, mybir.dt.from_np(v.dtype), kind="ExternalInput").ap()
          for k, v in arrays.items()}
    out = nc.dram_tensor("out", (1, T, D), F32, kind="ExternalOutput").ap()
    flamingo(nc, ap["x"], ap["ctx_t"], ap["wq"], ap["bqk"], ap["wk"], ap["wv"], ap["bv"], ap["w1"], ap["b1"],
             ap["w2"], ap["b2"], ap["wg"], ap["bg"], ap["gates"], (ap["ew1"], ap["ew2"], ap["ew3"]), ap["eb"],
             out.rearrange("o t d -> (o t) d"))
    result = run_bass_kernel_spmd(nc, [{"in_" + k: v for k, v in arrays.items()}], core_ids=[0])
    return result.results[0]["out"]
```

```python
import concourse.bass as bass
from concourse import mybir
from contextlib import ExitStack

F32, BF16, U32, I32 = mybir.dt.float32, mybir.dt.bfloat16, mybir.dt.uint32, mybir.dt.int32
ALU, ACT, AX = mybir.AluOpType, mybir.ActivationFunctionType, mybir.AxisListType

T, D, C, S = 2048, 256, 192, 1601
H, DH = 16, 16
FF = 2 * D
EX, TOP = 16, 64
EPS = 1e-5
SCALE = 1.0 / DH ** 0.5

QB = 512
NB = T // QB
HG = 4
NG = H // HG
STEPS = NB * NG
QT = QB // 128
KT = -(-S // 128)
KLAST = S - (KT - 1) * 128
TILES = HG * KT
RING = 3
KC = -(-S // 4)
CHUNKS = [(c * KC, min(KC, S - c * KC)) for c in range(4)]
QCHUNKS = HG * 4
ACH = QT * QCHUNKS
LEAD = 1
PARTS = 3 * DH * 2
HM = 8
CH = C // 2

K_WORDS, Q_WORDS, V_WORDS = HG * S // 2, HG * QB // 2, KT * HG * (DH + 1)
GROUP_WORDS = K_WORDS + Q_WORDS + V_WORDS
EXPERT_WORDS = 2 * D
FIT = [0, 0, 2 * GROUP_WORDS // EXPERT_WORDS, 3 * GROUP_WORDS // EXPERT_WORDS, 3 * EX]

PROJ = ([("k", 0, c, n) for c, n in CHUNKS] + [("q", 0, 0, QB)] + [("k", 1, c, n) for c, n in CHUNKS]
        + [("q", 1, 0, QB)] + [("q", m, b * QB, QB) for b in range(1, NB) for m in (0, 1)])
NPROJ = len(PROJ)
DVE_SPLITS = 5
STORES = {"k": 1, "q": 3}

MLP_UNITS = [(3, "bc0"), (4, "bc1"), (5, "w1_0"), (6, "w1_1"), (7, "w1_2"), (8, "w1_3"),
             (9, "w2_0"), (10, "w2_1"), (11, "w2_2"), (12, "w2_3")]
LN_UNITS = [(4, "tr0"), (5, "tr1"), (7, "lg")]
NEG_AT = 10


def plan(n):
    units = []
    if n >= NG:
        units += MLP_UNITS if n % NG == 0 else LN_UNITS if n % NG == 1 else []
    if n < STEPS - 1:
        units = units + [(NEG_AT, "neg")]
    return sorted(units, key=lambda u: u[0])


def spare_bank_order():
    order = [("neg", 0)]
    for n in range(STEPS):
        order += [("neg", n + 1) if u == "neg" else (u, n // NG - 1) for _, u in plan(n)]
    order += [(u, NB - 1) for _, u in MLP_UNITS + LN_UNITS]
    return {key: k for k, key in enumerate(order)}


ORDER = spare_bank_order()
USES_PER_BLOCK = NG + len(MLP_UNITS) + len(LN_UNITS)


def expert_dmas(layer):
    cuts = sorted({4 * k for k in range(3 * EX // 4)} | {f for f in FIT if f < 3 * EX})
    return sum(layer * EX <= c < (layer + 1) * EX for c in cuts)


def ring_wait(j, per_step):
    if j >= RING:
        return j - RING + 1
    return max(k for k in range(per_step) if k % RING == j) + 1 - per_step


class Step:

    def __init__(self, n0, r=None):
        self.n0, self.r, self.g = n0, r, n0 % NG

    def after(self, k):
        return Step(self.n0 + k, self.r)

    def count(self, per_step, plus=0):
        const = per_step * self.n0 + plus
        return const if self.r is None else self.r * (per_step * NG) + const

    def use(self, unit):
        k = ORDER[(unit, self.n0 if unit == "neg" else self.n0 // NG)]
        return k if self.r is None else self.r * USES_PER_BLOCK + k

    def block(self, plus=0, scale=1):
        const = (self.n0 // NG + plus) * scale
        return const if self.r is None else self.r * scale + const

    def halves(self, scale):
        const = self.n0 // 2 * scale
        return const if self.r is None else self.r * (NG // 2 * scale) + const


def wait(eng, sem, value):
    if not isinstance(value, int) or value > 0:
        eng.wait_ge(sem, value)


def run_steps(eng, step):
    for n in (0, 1):
        step(Step(n))
    with eng.Fori(0, NB - 1) as r:
        for n in range(2, 2 + NG):
            step(Step(n, r))
    for n in (STEPS - 2, STEPS - 1):
        step(Step(n))


def row_max_chunks(n0):
    out = []
    for q in range(QT):
        ahead, t = 1 + (q + LEAD) // QT, (q + LEAD) % QT
        if n0 + ahead < STEPS:
            out += [(ahead, t, h, c) for h in range(HG) for c in range(4)]
    return out


def flamingo(nc, ident_c, spread_c, ones_c, ones_row, x, ctx_t, wq, b_qk, wk, wv, bv, w1, b1, w2, b2, wg, bg, gates, ew, eb, out):
    es = ExitStack()
    with es:
        def sb(name, shape, dt):
            return es.enter_context(nc.sbuf_tensor(name, shape, dt))

        def pb(name, shape, dt):
            return es.enter_context(nc.psum_tensor(name, shape, dt))

        def sem(name):
            return es.enter_context(nc.semaphore(name))

        def dram(name, shape, dt):
            return nc.dram_tensor(name, shape, dt, kind="Internal").ap()

        region = sb("region", [128, 3 * EX * 2 * D], F32)
        k_rows, q_rows, v_cols = [], [], []
        for g in range(NG):
            at = g * GROUP_WORDS
            k_rows.append(region[:, at:at + K_WORDS].bitcast(BF16).rearrange("p (h s) -> p h s", h=HG))
            at += K_WORDS
            q_rows.append(region[:, at:at + Q_WORDS].bitcast(BF16).rearrange("p (h n) -> p h n", h=HG))
            at += Q_WORDS
            v_cols.append(region[:, at:at + V_WORDS].rearrange("p (k h d) -> p k h d", k=KT, h=HG))
        p_flat = region[:, NG * GROUP_WORDS:NG * GROUP_WORDS + 2 * HG * QB]
        probs = p_flat.rearrange("p (s h n) -> p s h n", s=2, h=HG)
        w_exp = region[:, :].rearrange("p (l e k o) -> p l e k o", l=3, e=EX, k=2)

        x_in = sb("x_in", [128, T // 128, D], F32)
        xn_t = sb("xn_t", [128, 2 * T], F32)
        xn_tv = xn_t[:, :].rearrange("p (k n) -> p k n", k=2)
        hidden = xn_t[:, 0:4 * QB].rearrange("p (m n) -> p m n", m=4)
        att_t = xn_t[:, 4 * QB:6 * QB].rearrange("p (k n) -> p k n", k=2)
        xn2_t = xn_t[:, 6 * QB:8 * QB].rearrange("p (k n) -> p k n", k=2)
        ctx_sb = sb("ctx_sb", [128, 2, S], F32)
        logits = ctx_sb[0:EX, :, :].rearrange("p k s -> p (k s)")[:, 0:T]
        wq_sb = sb("wq_sb", [128, 2, D], F32)
        wk_sb = sb("wk_sb", [CH, 2, D], F32)
        wv_sb = sb("wv_sb", [CH + 1, 2, D], F32)
        bqk = sb("bqk", [128, 2, 2], F32)
        w1_sb = sb("w1_sb", [128, 2, FF], F32)
        b1_sb = sb("b1_sb", [128, 4], F32)
        w2_sb = sb("w2_sb", [128, 4, D], F32)
        b2_sb = sb("b2_sb", [128, D], F32)
        wg_sb = sb("wg_sb", [128, 2, EX], F32)
        bg_sb = sb("bg_sb", [EX, 1], F32)
        eb_sb = sb("eb_sb", [128, 3, EX // 2], F32)
        gate_in = sb("gate_in", [128, 2], F32)
        gate = sb("gate", [128, 2], F32)
        eps = sb("eps", [128, 1], F32)
        ident = sb("ident", [128, 128], F32)
        spread = sb("spread", [128, 2, 128], F32)
        stats = sb("stats", [128, T // 128, 6], F32)
        moments = sb("moments", [128, T // 128, 2], F32)
        std = sb("std", [128, T // 128], F32)
        carrier = sb("carrier", [128, 1], F32)
        rstd = sb("rstd", [128, T // 128], F32)
        x2 = sb("x2", [128, QT, D], F32)
        xn2 = sb("xn2", [128, QT, D], F32)
        att_raw = sb("att_raw", [128, 2, QB], F32)
        den = sb("den", [128, QB], F32)
        rden = sb("rden", [128, QB], F32)
        pv_raw = sb("pv_raw", [128, 2, QB], F32)
        cmax = sb("cmax", [128, 2, HG * QT * 4], F32)
        negmax = sb("negmax", [128, 2, HG * QT], F32)
        neg_parts = sb("neg_parts", [HG * QT, 3, 128], BF16)
        neg_rest = sb("neg_rest", [HG * QT, 128], F32)
        split_g = sb("split_g", [128, 2, 7 * QB // 2], F32)

        def split_bufs(buf):
            return (buf[:, 0:QB], buf[:, QB:2 * QB],
                    buf[:, 2 * QB:2 * QB + 3 * QB // 2].bitcast(BF16).rearrange("p (j n) -> p j n", j=3))

        SPLIT = ([split_bufs(p_flat[:, i * 2 * QB * 2:(i * 2 + 2) * 2 * QB]) for i in range(2)],
                 [split_bufs(split_g[:, i, :]) for i in range(2)])

        q_scr = [dram(f"q_scr{m}", [6, 128, T], BF16) for m in range(2)]
        k_scr = [dram(f"k_scr{m}", [3, 128, S], BF16) for m in range(2)]
        xn2_scr = dram("xn2_scr", [T, D], F32)
        logit_scr = dram("logit_scr", [EX, T], F32)
        cand_scr = dram("cand_scr", [128, TOP], F32)
        cand_id_scr = dram("cand_id_scr", [128 * TOP, 1], U32)
        place_scr = dram("place_scr", [EX, TOP], U32)
        weight_scr = dram("weight_scr", [EX, TOP], F32)
        token_scr = dram("token_scr", [EX // 2, 128], U32)

        ps_s = pb("ps_s", [128, RING, 512], F32)
        ps_a = pb("ps_a", [128, RING, 512], F32)
        ps_v = pb("ps_v", [128, 512], F32)
        ps_m = pb("ps_m", [128, 512], F32)

        ctx_in, x_loaded, q_in, v_in, mlp_in = sem("ctx_in"), [sem(f"x_loaded{b}") for b in range(NB)], \
            sem("q_in"), sem("v_in"), sem("mlp_in")
        gates_in, gates_ready = sem("gates_in"), sem("gates_ready")
        eps_ready, ident_in, ones_in, v_ones, rden_zero = (
            sem("eps_ready"), sem("ident_in"), sem("ones_in"), sem("v_ones"), sem("rden_zero"))
        b2_scaled, x_biased = sem("b2_scaled"), sem("x_biased")
        ln_stat, ln_mean, ln_std, ln_rstd, ln_out = (
            sem("ln_stat"), sem("ln_mean"), sem("ln_std"), sem("ln_rstd"), sem("ln_out"))
        xt_filled, xt_free = sem("xt_filled"), sem("xt_free")
        proj_filled, proj_free, part1_ready = sem("proj_filled"), sem("proj_free"), sem("part1_ready")
        part2_ready = sem("part2_ready")
        split_v, split_g_s = sem("split_v"), sem("split_g_s")
        stored = [sem(f"stored{c}") for c in range(NPROJ)]
        k_relaid = [sem(f"k_relaid{g}") for g in range(NG)]
        q_loaded = [sem(f"q_loaded{g}") for g in range(NG)]
        a_filled, a_free, neg_ready = sem("a_filled"), sem("a_free"), sem("neg_ready")
        spare_filled, spare_free = sem("spare_filled"), sem("spare_free")
        neg_split, neg_rows = sem("neg_split"), sem("neg_rows")
        scores_ready, exp_done, pv_done, pv_out = (
            sem("scores_ready"), sem("exp_done"), sem("pv_done"), sem("pv_out"))
        att_moved, rden_ready = [sem(f"att_moved{i}") for i in range(2)], sem("rden_ready")
        x2_stored, xn2_stored, logit_stored = sem("x2_stored"), sem("xn2_stored"), sem("logit_stored")

        cand_space = sb("cand_space", [128, 1024], F32)
        chunk_logits = cand_space[:, 0:256]
        cand = cand_space[:, 256:256 + TOP]
        cand_pos = cand_space[:, 320:384].bitcast(U32)
        cand_id = cand_space[:, 384:448].bitcast(U32)
        cand_e = cand_space[0:EX, 448:448 + 8 * TOP]
        top_v = sb("top_v", [EX, TOP], F32)
        top_pos = sb("top_pos", [EX, TOP], U32)
        place_id = sb("place_id", [EX, TOP], U32)
        weight = sb("weight", [EX, TOP], F32)
        small = sb("small", [128, 8], F32)
        part_no = sb("part_no", [128, 1], I32)
        part_and = sb("part_and", [128, 1], I32)
        place_slot = sb("place_slot", [128, EX // 2], U32)
        weight_slot = sb("weight_slot", [128, EX // 2], F32)
        token_slot = sb("token_slot", [128, EX // 2], U32)
        token_exp = sb("token_exp", [TOP, EX], U32)
        tok_x = x_in[:, 0:EX // 2, :]
        h_in = xn_t[:, 0:8 * D].rearrange("p (a k n) -> p a k n", a=EX // 2, k=2)
        h_out = xn_t[:, 8 * D:16 * D].rearrange("p (a n) -> p a n", a=EX // 2)
        y_out = x_in[:, EX // 2:EX, :]
        w_in = [sem(f"w_in{l}") for l in range(3)]
        chunk_in, cand_ready, cand_stored, cand_id_stored, cand_e_in = (
            sem("chunk_in"), sem("cand_ready"), sem("cand_stored"), sem("cand_id_stored"), sem("cand_e_in"))
        offs_ready, top_step, place_ready, place_stored, place_in = (
            sem("offs_ready"), sem("top_step"), sem("place_ready"), sem("place_stored"), sem("place_in"))
        sum_ready, weight_ready, weight_stored, weight_in = (
            sem("sum_ready"), sem("weight_ready"), sem("weight_stored"), sem("weight_in"))
        negtop_ready, top_exp = sem("negtop_ready"), sem("top_exp")
        token_in = [sem(f"token_in{a}") for a in range(EX // 2)]
        token_stored, token_exp_in = sem("token_stored"), sem("token_exp_in")
        x_gathered = [sem(f"x_gathered{a}") for a in range(EX // 2)]
        t_filled, t_free, l_filled, l_free = sem("t_filled"), sem("t_free"), sem("l_filled"), sem("l_free")
        scattered = sem("scattered")
        chunk_off = small[:, 0:1]
        exp_off = small[0:EX, 1:2]
        neg_top = small[0:EX, 2:3]
        exp_sum = small[0:EX, 3:4]
        exp_rsum = small[0:EX, 4:5]
        ps_t = [ps_a[:, 0, :], ps_a[:, 1, :], ps_v[:, :], ps_m[:, :]]
        ps_l = [ps_s[:, 0, :], ps_s[:, 1, :], ps_s[:, 2, :], ps_a[:, 2, :]]
        tail_banks = [ps_m[:, :], ps_a[:, 0, :], ps_a[:, 1, :], ps_a[:, 2, :]]
        HALF = EX // 4

        block = es.enter_context(nc.Block())
        SPLITS_OF = lambda c: (0, c) if c < DVE_SPLITS else (1, c - DVE_SPLITS)

        NEG_DMAS, ATT_DMAS = 3 * 16, (HG + 1) * 16

        def bank(s, name):
            return ps_m[:, :] if s.n0 < STEPS else tail_banks[int(name[-1]) if name != "lg" else 0]

        def first_of(name):
            return name[:-1] + "0" if name != "lg" else name

        @block.sync
        def _(sp):
            for k in range(2):
                sp.dma_start(ctx_sb[0:CH, k, :], ctx_t[k * CH:(k + 1) * CH, :]).then_inc(ctx_in, 16)
                if k == 0:
                    sp.dma_start(wk_sb[:, :, :], wk.rearrange("(k p) o -> p k o", k=2)).then_inc(ctx_in, 16)

            def load_x(b):
                sp.dma_start(x_in[:, b * QT:(b + 1) * QT, :],
                             x[b * QB:(b + 1) * QB, :].rearrange("(t p) d -> p t d", p=128)
                             ).then_inc(x_loaded[b], 16)

            load_x(0)
            sp.dma_start(ident[:, :], ident_c).then_inc(ident_in, 16)
            sp.dma_start(gate_in[:, :], gates).then_inc(gates_in, 16)
            sp.dma_start(bqk[:, :, :], b_qk).then_inc(ctx_in, 16)
            sp.dma_start(wq_sb[:, :, :], wq.rearrange("(k p) o -> p k o", k=2)).then_inc(q_in, 16)
            load_x(1)

            def load_later():
                load_x(2)
                load_x(3)
                for g in range(NG):
                    sp.dma_start(k_rows[g][PARTS:PARTS + 3, :, :].rearrange("p h s -> p (h s)"), ones_c
                                 ).then_inc(ones_in, 16)
                sp.dma_start(wv_sb[0:CH, :, :], wv.rearrange("(k p) o -> p k o", k=2)).then_inc(v_in, 16)
                sp.dma_start(wv_sb[CH:CH + 1, 1, :], bv).then_inc(v_in, 16)
                sp.dma_start(ctx_sb[CH:CH + 1, 1, :], ones_row).then_inc(v_in, 16)
                sp.dma_start(spread[:, :, :], spread_c).then_inc(mlp_in, 16)
                sp.dma_start(b2_sb[:, :], b2).then_inc(mlp_in, 16)
                sp.dma_start(w1_sb[:, :, :], w1.rearrange("(k p) o -> p k o", k=2)).then_inc(mlp_in, 16)
                sp.dma_start(b1_sb[:, :], b1).then_inc(mlp_in, 16)
                sp.dma_start(w2_sb[:, :, :], w2.rearrange("(k p) o -> p k o", k=4)).then_inc(mlp_in, 16)
                sp.dma_start(wg_sb[:, :, :], wg.rearrange("(k p) o -> p k o", k=2)).then_inc(mlp_in, 16)
                sp.dma_start(bg_sb[:, :], bg).then_inc(mlp_in, 16)
                sp.dma_start(eb_sb[:, :, :], eb).then_inc(mlp_in, 16)

            def store(c):
                kind, m, c0, n = PROJ[c]
                eng, i = SPLITS_OF(c)
                parts = SPLIT[eng][i % 2][2]
                sp.wait_ge((split_v, split_g_s)[eng], (3, 2)[eng] * (i + 1))
                if kind == "k":
                    sp.dma_start(k_scr[m][:, :, c0:c0 + n].rearrange("j p n -> p j n"),
                                 parts[:, :, 0:n]).then_inc(stored[c], 16)
                else:
                    for j, (lo, hi) in enumerate(((0, 3), (3, 5), (5, 6))):
                        sp.dma_start(q_scr[m][lo:hi, :, c0:c0 + n].rearrange("j p n -> p j n"),
                                     parts[:, j:j + 1, 0:n].broadcast_to([128, hi - lo, n])
                                     ).then_inc(stored[c], 16)

            def relay_k(m):
                for c in range(NPROJ):
                    if PROJ[c][:2] == ("k", m):
                        sp.wait_ge(stored[c], 16)
                for g in range(2):
                    for row, parts in ((0, 3), (3, 2), (5, 1)):
                        src = k_scr[m][0:parts, :, :].rearrange("j (d h) n -> (j d) h n", h=HM)
                        sp.dma_start(k_rows[2 * m + g][row * DH:(row + parts) * DH, :, :],
                                     src[:, g * HG:(g + 1) * HG, :]).then_inc(k_relaid[2 * m + g], 16)

            def load_q(s):
                m, h0 = s.g * HG // HM, s.g * HG % HM
                sp.dma_start(q_rows[s.g][0:PARTS, :, :],
                             q_scr[m].rearrange("j (d h) n -> (j d) h n", h=HM)
                             [:, h0:h0 + HG, bass.ds(s.block(scale=QB), QB)]).then_inc(q_loaded[s.g], 16)

            def put_neg(s):
                sp.wait_ge(neg_split, s.count(3, 3))
                for j in range(3):
                    sp.dma_start(q_rows[s.g][PARTS + j:PARTS + j + 1, :, :].rearrange("p h n -> p (h n)"),
                                 neg_parts[:, j, :]).then_inc(neg_rows, 16)

            def move_attention(s):
                wait(sp, pv_out, s.count(1, 1))
                if s.g == 0 and s.n0 >= NG:
                    wait(sp, spare_free, Step(s.n0 - NG, s.r).use("bc1") + 1)
                for h in range(HG):
                    r0 = (s.g % 2) * HG * DH + h * DH
                    sp.dma_start(att_raw[r0:r0 + DH, s.g // 2, :],
                                 pv_raw[32 * h:32 * h + DH, s.g % 2, :]).then_inc(att_moved[s.g % 2], 16)
                sp.dma_start(den[s.g * HG:(s.g + 1) * HG, :],
                             pv_raw[DH:128:32, s.g % 2, :]).then_inc(att_moved[s.g % 2], 16)

            def store_x2(b):
                wait(sp, spare_free, b.use("w2_3") + 1)
                sp.dma_start(out[bass.ds(b.block(scale=QB), QB), :].rearrange("(t p) d -> p t d", p=128),
                             x2[:, :, :]).then_inc(x2_stored, 16)

            def store_xn2(b):
                wait(sp, ln_out, b.block(1, QT) + NB * QT)
                sp.dma_start(xn2_scr[bass.ds(b.block(scale=QB), QB), :].rearrange("(t p) d -> p t d", p=128),
                             xn2[:, :, :]).then_inc(xn2_stored, 16)

            def store_logits(b):
                wait(sp, spare_free, b.use("lg") + 1)
                sp.dma_start(logit_scr[:, bass.ds(b.block(scale=QB), QB)],
                             logits[:, bass.ds(b.block(scale=QB), QB)]).then_inc(logit_stored, 16)

            first_second_half = next(c for c in range(NPROJ) if PROJ[c][:2] == ("q", 1))
            for c in range(first_second_half + 1):
                store(c)
                if PROJ[c][0] == "k" and PROJ[c + 1][0] == "q":
                    relay_k(PROJ[c][1])
                if c == 4:
                    sp.wait_ge(stored[c], 48)
                    load_q(Step(0))
                    load_q(Step(1))
                    load_later()
            sp.wait_ge(stored[first_second_half], 48)
            for c in range(first_second_half + 1, NPROJ):
                store(c)
            put_neg(Step(0))

            def load_experts(groups, upto):
                for u in range(FIT[groups], FIT[upto]):
                    l, e = u // EX, u % EX
                    if u == FIT[groups] or e == 0 or e % 4 == 0:
                        n = min(4 - e % 4, FIT[upto] - u)
                        sp.dma_start(w_exp[:, l, e:e + n, :, :].rearrange("p e k o -> p (e k) o"),
                                     ew[l][e:e + n, :, :].rearrange("e (k p) o -> p (e k) o", k=2)
                                     ).then_inc(w_in[l], 16)

            def step(s):
                if s.n0 >= 1:
                    move_attention(s.after(-1))
                if s.n0 == STEPS - 2:
                    load_experts(0, 2)
                if s.n0 == STEPS - 1:
                    load_experts(2, 3)
                if s.n0 == 1:
                    for c in range(first_second_half + 1, NPROJ):
                        sp.wait_ge(stored[c], 48)
                prev = Step(s.n0 - NG, s.r)
                if s.n0 > NG and s.g == 1:
                    store_x2(prev)
                if s.n0 + 2 < STEPS:
                    wait(sp, scores_ready, s.count(TILES, -TILES))
                    load_q(s.after(2))
                if s.n0 > NG and s.g == 1:
                    store_xn2(prev)
                    store_logits(prev)
                if s.n0 + 1 < STEPS:
                    put_neg(s.after(1))

            run_steps(sp, step)
            last = Step(STEPS - 1)
            move_attention(last)

            load_experts(3, 4)
            store_x2(last)
            store_xn2(last)
            store_logits(last)
            sp.wait_ge(logit_stored, 16 * NB)
            sp.dma_start(chunk_logits[:, :], logit_scr.rearrange("e (c n) -> (e c) n", c=8)
                         ).then_inc(chunk_in, 16)
            sp.wait_ge(cand_ready, 25)
            sp.dma_start(cand_scr, cand[:, :]).then_inc(cand_stored, 16)
            sp.dma_start(cand_id_scr.rearrange("(p n) o -> p (n o)", p=128), cand_id[:, :]
                         ).then_inc(cand_id_stored, 16)
            sp.wait_ge(cand_stored, 16)
            sp.dma_start(cand_e[:, :], cand_scr.rearrange("(e c) n -> e (c n)", e=EX)).then_inc(cand_e_in, 16)
            sp.wait_ge(place_ready, 1)
            sp.dma_start(place_scr, place_id[:, :]).then_inc(place_stored, 16)
            sp.wait_ge(place_stored, 16)
            sp.dma_start(place_slot[:, :], place_scr.rearrange("(a h) j -> (h j) a", h=2), allow_slow_non_contiguous=True
                         ).then_inc(place_in, 16)
            sp.wait_ge(weight_ready, 2)
            sp.dma_start(weight_scr, weight[:, :]).then_inc(weight_stored, 16)
            sp.wait_ge(weight_stored, 16)
            sp.dma_start(weight_slot[:, :], weight_scr.rearrange("(a h) j -> (h j) a", h=2), allow_slow_non_contiguous=True
                         ).then_inc(weight_in, 16)
            for a in range(EX // 2):
                sp.wait_ge(token_in[a], 16)
            sp.dma_start(token_scr.rearrange("a p -> p a"), token_slot[:, :], allow_slow_non_contiguous=True).then_inc(token_stored, 16)
            sp.wait_ge(token_stored, 16)
            sp.dma_start(token_exp[:, :], token_scr.rearrange("a (h j) -> j (a h)", h=2), allow_slow_non_contiguous=True
                         ).then_inc(token_exp_in, 16)


        @block.gpsimd
        def _(pool):
            def split(c):
                kind, m, c0, n = PROJ[c]
                i = c - DVE_SPLITS
                full, rest, parts = SPLIT[1][i % 2]
                pool.wait_ge(part1_ready, c + 1)
                pool.tensor_tensor(out=rest[:, 0:n], in0=full[:, 0:n], in1=parts[:, 0, 0:n],
                                   op=ALU.subtract).then_inc(split_g_s, 1)
                pool.wait_ge(part2_ready, i + 1)
                pool.tensor_tensor(out=parts[:, 2, 0:n], in0=rest[:, 0:n], in1=parts[:, 1, 0:n],
                                   op=ALU.subtract).then_inc(split_g_s, 1)

            for c in range(DVE_SPLITS, NPROJ):
                split(c)
            pool.wait_ge(b2_scaled, 1)
            for t in range(T // 128):
                if t == 0:
                    pool.wait_ge(ln_out, T // 128)
                pool.tensor_tensor(out=x_in[:, t, :], in0=x_in[:, t, :], in1=b2_sb[:, :],
                                   op=ALU.add).then_inc(x_biased, 1)
            pool.iota(part_no[:, :], [[0, 1]], base=0, channel_multiplier=1).then_inc(offs_ready, 1)

            pool.wait_ge(place_in, 16)
            pool.wait_ge(cand_id_stored, 16)
            for a in range(EX // 2):
                pool.indirect_dma_start(token_slot[:, a:a + 1], None, cand_id_scr,
                                        bass.IndirectOffsetOnAxis(place_slot[:, a:a + 1], 0),
                                        bounds_check=128 * TOP - 1).then_inc(token_in[a], 16)
            pool.wait_ge(xn2_stored, 16 * NB)
            pool.wait_ge(spare_free, ORDER[("w2_3", NB - 1)] + 1)
            for a in range(EX // 2):
                pool.wait_ge(token_in[a], 16)
                pool.indirect_dma_start(tok_x[:, a, :], None, xn2_scr,
                                        bass.IndirectOffsetOnAxis(token_slot[:, a:a + 1], 0),
                                        bounds_check=T - 1).then_inc(x_gathered[a], 16)
            pool.wait_ge(token_exp_in, 16)
            pool.wait_ge(x2_stored, 16 * NB)
            for e in range(EX):
                a = e // 2
                g, a4 = a // HALF, a % HALF
                pool.wait_ge(l_free, (g * 3 + 2) * HALF + a4 + 1)
                if e:
                    pool.wait_ge(scattered, 16 * e)
                r0 = (e % 2) * TOP
                pool.indirect_dma_start(out, bass.IndirectOffsetOnAxis(token_exp[:, e:e + 1], 0),
                                        y_out[r0:r0 + TOP, a, :], None, compute_op=ALU.add,
                                        bounds_check=T - 1).then_inc(scattered, 16)
            pool.wait_ge(scattered, 16 * EX)

        @block.scalar
        def _(act):
            act.wait_ge(eps_ready, 1)

            def block_std(b):
                act.wait_ge(ln_mean, QT * (b + 1))
                tiles = slice(b * QT, (b + 1) * QT)
                act.activation(std[:, tiles], moments[:, tiles, 1], ACT.Sqrt, bias=eps[:, :]).then_inc(ln_std, 1)

            def transposed_x(b):
                for k in range(2):
                    act.wait_ge(xt_filled, 2 * b + k + 1)
                    act.activation(xn_tv[:, k, b * QB:(b + 1) * QB], (ps_m if k == 0 else ps_v)[:, :],
                                   ACT.Copy).then_inc(xt_free, 1)

            def projected(c):
                kind, m, c0, n = PROJ[c]
                eng, i = SPLITS_OF(c)
                full, _, parts = SPLIT[eng][i % 2]
                act.wait_ge(proj_filled, c + 1)
                if i >= 2:
                    act.wait_ge(stored[c - 2], 16 * STORES[PROJ[c - 2][0]])
                act.activation(full[:, 0:n], ps_s[:, c % RING, 0:n], ACT.Identity,
                               bias=bqk[:, 0 if kind == "q" else 1, m:m + 1]).then_inc(proj_free, 1)
                act.wait_ge(proj_free, c + 1)
                act.activation(parts[:, 0, 0:n], full[:, 0:n], ACT.Copy).then_inc(part1_ready, 1)
                if c > DVE_SPLITS:
                    second_part(c - 1)

            def second_part(c):
                i, n = c - DVE_SPLITS, PROJ[c][3]
                _, rest, parts = SPLIT[1][i % 2]
                act.wait_ge(split_g_s, 2 * i + 1)
                act.activation(parts[:, 1, 0:n], rest[:, 0:n], ACT.Copy).then_inc(part2_ready, 1)

            def values(v):
                keys = 128 if v < KT - 1 else KLAST
                act.wait_ge(proj_filled, NPROJ + v + 1)
                if v == 0:
                    act.wait_ge(v_ones, NG)
                for g in range(NG):
                    cols = slice(g * HG * DH, (g + 1) * HG * DH)
                    last = act.activation(v_cols[g][0:keys, v, :, 0:DH],
                                          ps_s[0:keys, (NPROJ + v) % RING, cols].rearrange("p (h d) -> p h d", h=HG),
                                          ACT.Copy)
                last.then_inc(proj_free, 1)

            act.wait_ge(gates_in, 16)
            act.activation(gate[:, :], gate_in[:, :], ACT.Tanh).then_inc(gates_ready, 1)
            act.wait_ge(ctx_in, 64)
            projected(0)
            block_std(0)
            for c in range(1, 4):
                projected(c)
            transposed_x(0)
            for what, i in PROLOGUE[5:]:
                if what == "proj":
                    projected(i)
                    if i == NPROJ - 1:
                        second_part(i)
                    if i == 8:
                        for b in range(1, NB):
                            block_std(b)
                elif what == "xt":
                    transposed_x(i)
                elif what == "v":
                    values(i)

            act.wait_ge(mlp_in, 16 * 8)

            def unit(s, name):
                b = Step(s.n0 - NG, s.r)
                ps_m = bank(s, name)
                if name.startswith("w1_"):
                    m = int(name[3])
                    wait(act, spare_filled, b.use(name) + 1)
                    act.activation(hidden[:, m, :], ps_m[:, :], ACT.Relu,
                                   bias=b1_sb[:, m:m + 1]).then_inc(spare_free, 1)
                elif name.startswith("tr"):
                    wait(act, spare_filled, b.use(name) + 1)
                    act.activation(xn2_t[:, int(name[2]), :], ps_m[:, :], ACT.Copy).then_inc(spare_free, 1)
                elif name == "lg":
                    wait(act, spare_filled, b.use(name) + 1)
                    act.activation(logits[:, bass.ds(b.block(scale=QB), QB)], ps_m[0:EX, :], ACT.Identity,
                                   bias=bg_sb[:, :]).then_inc(spare_free, 1)

            def router_std(b):
                wait(act, ln_mean, b.block(1, QT) + NB * QT)
                act.activation(std[:, 0:QT], moments[:, 0:QT, 1], ACT.Sqrt, bias=eps[:, :]).then_inc(ln_std, 1)

            def pv_copy(s):
                wait(act, pv_done, s.count(KT, KT))
                if s.n0 >= 2:
                    wait(act, att_moved[s.g % 2], s.halves(ATT_DMAS))
                act.activation(pv_raw[:, s.g % 2, :], ps_v[:, :], ACT.Copy).then_inc(pv_out, 1)

            def step(s):
                units = dict()
                for kt, name in plan(s.n0):
                    units.setdefault(kt, []).append(name)
                for kt in range(KT):
                    keys = 128 if kt < KT - 1 else KLAST
                    for h in range(HG):
                        j = HG * kt + h
                        wait(act, scores_ready, s.count(TILES, j + 1))
                        if h == 0 and s.n0 * KT + kt >= 2:
                            wait(act, pv_done, s.count(KT, kt - 1))
                        act.activation(probs[0:keys, (s.g * KT + kt) % 2, h, :], ps_s[0:keys, j % RING, :], ACT.Exp,
                                       scale=SCALE).then_inc(exp_done, 1)
                    if kt == 0 and s.n0 >= 1:
                        pv_copy(s.after(-1))
                    if kt == 1 and s.n0 > NG and s.g == 1:
                        router_std(Step(s.n0 - NG, s.r))
                    for name in units.get(kt, []):
                        unit(s, name)

            run_steps(act, step)
            last = Step(STEPS - 1)
            pv_copy(last)
            past = Step(STEPS)
            for _, name in MLP_UNITS:
                unit(past, name)
            router_std(last)
            for _, name in LN_UNITS:
                unit(past, name)

            act.wait_ge(negtop_ready, 1)
            act.wait_ge(spare_free, len(ORDER))
            act.activation(xn_t[0:EX, 0:T], logits[:, :], ACT.Exp, bias=neg_top,
                           accum_out=exp_sum).then_inc(sum_ready, 1)
            act.wait_ge(place_ready, 1)
            act.activation(weight[:, :], top_v[:, :], ACT.Exp, bias=neg_top).then_inc(top_exp, 1)
            for g in range(2):
                for l in range(2):
                    for a4 in range(HALF):
                        a = g * HALF + a4
                        q = (g * 3 + l) * HALF + a4
                        act.wait_ge(l_filled, q + 1)
                        act.activation(h_out[:, a, :], ps_l[a4][:, 0:D], ACT.Relu,
                                       bias=eb_sb[:, l, a:a + 1]).then_inc(l_free, 1)
                for a4 in range(HALF):
                    q = (g * 3 + 2) * HALF + a4
                    act.wait_ge(l_free, q + 1)

        @block.vector
        def _(dve):
            dve.memset(eps[:, :], EPS).then_inc(eps_ready, 1)

            def moments_of(src, base, t0=0):
                for t in range(QT):
                    dve.bn_stats(stats[:, t0 + t, :], src[:, t, :]).then_inc(ln_stat, 1)
                wait(dve, ln_stat, base + QT)
                if not isinstance(base, int):
                    dve.memset(carrier[:, :], 0.0)
                for t in range(QT):
                    dve.bn_aggr(moments[:, t0 + t, :], stats[:, t0 + t, :]).then_inc(ln_mean, 1)

            def normalise(src, blocks_before, t0=0):
                wait(dve, ln_std, blocks_before + 1)
                dve.reciprocal(rstd[:, t0:t0 + QT], std[:, t0:t0 + QT]).then_inc(ln_rstd, 1)
                wait(dve, ln_rstd, blocks_before + 1)
                for t in range(QT):
                    dve.tensor_scalar(xn2[:, t, :], src[:, t, :], moments[:, t0 + t, 0:1], rstd[:, t0 + t:t0 + t + 1],
                                      ALU.subtract, ALU.mult).then_inc(ln_out, 1)

            def split(c):
                kind, m, c0, n = PROJ[c]
                full, rest, parts = SPLIT[0][c % 2]
                dve.wait_ge(part1_ready, c + 1)
                dve.tensor_tensor(out=rest[:, 0:n], in0=full[:, 0:n], in1=parts[:, 0, 0:n],
                                  op=ALU.subtract).then_inc(split_v, 1)
                dve.wait_ge(split_v, 3 * c + 1)
                dve.tensor_copy(parts[:, 1, 0:n], rest[:, 0:n]).then_inc(split_v, 1)
                dve.wait_ge(split_v, 3 * c + 2)
                dve.tensor_tensor(out=parts[:, 2, 0:n], in0=rest[:, 0:n], in1=parts[:, 1, 0:n],
                                  op=ALU.subtract).then_inc(split_v, 1)

            def x_moments(b):
                dve.wait_ge(x_loaded[b], 16)
                moments_of(x_in[:, b * QT:(b + 1) * QT, :], QT * b, QT * b)

            def x_normal(b):
                if b:
                    dve.wait_ge(xt_filled, 2 * b)
                dve.wait_ge(ln_mean, QT * (b + 1))
                normalise(x_in[:, b * QT:(b + 1) * QT, :], b, QT * b)

            dve.memset(rden[:, :], 0.0).then_inc(rden_zero, 1)
            for g in range(NG):
                dve.memset(v_cols[g][:, :, :, DH:DH + 1], 1.0).then_inc(v_ones, 1)
            x_moments(0)
            split(0)
            x_normal(0)
            for c in range(1, 5):
                split(c)
            for b in range(1, NB):
                x_moments(b)

            def row_max(s, t, h, c):
                g_local = (t * HG + h) * 4 + c
                if g_local == 0 and s.n0 >= 2:
                    wait(dve, neg_ready, s.count(1, -1))
                wait(dve, a_filled, s.count(ACH, g_local + 1))
                col = (h * QT + t) * 4 + c
                dve.reduce_max(cmax[:, s.g % 2, col:col + 1], ps_a[:, g_local % RING, 0:CHUNKS[c][1]],
                               AX.X).then_inc(a_free, 1)

            def neg_max(s):
                wait(dve, a_free, s.count(ACH, ACH))
                if s.n0 >= 2:
                    wait(dve, spare_filled, Step(s.n0 - 2, s.r).use("neg") + 1)
                dve.tensor_reduce(out=negmax[:, s.g % 2, :],
                                  in_=cmax[:, s.g % 2, :].rearrange("p (u c) -> p u c", c=4),
                                  axis=AX.X, op=ALU.max, negate=True).then_inc(neg_ready, 1)

            def neg_to_parts(s):
                wait(dve, spare_filled, s.use("neg") + 1)
                if s.n0 >= 1:
                    wait(dve, neg_rows, s.count(NEG_DMAS))
                dve.tensor_copy(neg_parts[:, 0, :], ps_m[0:HG * QT, 0:128]).then_inc(neg_split, 1)
                wait(dve, neg_split, s.count(3, 1))
                dve.tensor_tensor(out=neg_rest[:, :], in0=ps_m[0:HG * QT, 0:128], in1=neg_parts[:, 0, :],
                                  op=ALU.subtract).then_inc(spare_free, 1)
                wait(dve, spare_free, s.use("neg") + 1)
                dve.tensor_copy(neg_parts[:, 1, :], neg_rest[:, :]).then_inc(neg_split, 1)
                wait(dve, neg_split, s.count(3, 2))
                dve.tensor_tensor(out=neg_parts[:, 2, :], in0=neg_rest[:, :], in1=neg_parts[:, 1, :],
                                  op=ALU.subtract).then_inc(neg_split, 1)

            def unit(s, name):
                b = Step(s.n0 - NG, s.r)
                ps_m = bank(s, name)
                if name == "neg":
                    neg_to_parts(s.after(1))
                elif name.startswith("bc"):
                    k = int(name[2])
                    wait(dve, spare_filled, b.use(name) + 1)
                    dve.tensor_tensor(out=att_t[:, k, :], in0=ps_m[:, :], in1=att_raw[:, k, :],
                                      op=ALU.mult).then_inc(spare_free, 1)
                elif name.startswith("w2_"):
                    t = int(name[3])
                    if t == 0 and s.n0 >= 2 * NG:
                        wait(dve, x2_stored, b.block(scale=16))
                    wait(dve, spare_filled, b.use(name) + 1)
                    if t == 0 and s.n0 == NG and s.r is None or t == 0:
                        dve.wait_ge(x_biased, T // 128)
                    dve.scalar_tensor_tensor(out=x2[:, t, :], in0=ps_m[:, 0:D], scalar=gate[:, 0:1],
                                             in1=x_in[:, bass.ds(b.block(scale=QT) + t, 1), :]
                                             .rearrange("p o d -> p (o d)"),
                                             op0=ALU.mult, op1=ALU.add).then_inc(spare_free, 1)

            def denominators(b):
                for parity in range(2):
                    wait(dve, att_moved[parity], b.block(1, NG // 2 * ATT_DMAS))
                dve.wait_ge(rden_zero, 1)
                dve.reciprocal(rden[0:H, :], den[0:H, :]).then_inc(rden_ready, 1)

            def router_moments(b):
                wait(dve, spare_free, b.use("w2_3") + 1)
                wait(dve, ln_out, b.block(0, QT) + NB * QT)
                wait(dve, ln_mean, b.block(0, QT) + NB * QT)
                moments_of(x2[:, :, :], b.block(0, QT) + NB * QT)

            def router_norm(b, first):
                if not first:
                    wait(dve, xn2_stored, b.block(scale=16))
                wait(dve, ln_mean, b.block(1, QT) + NB * QT)
                normalise(x2[:, :, :], b.block() + NB)

            def between(s, kt, done):
                prev = Step(s.n0 - NG, s.r)
                if s.n0 >= NG and s.g == 0 and kt == 2:
                    denominators(prev)
                if s.n0 > NG and s.g == 1 and kt == 0:
                    router_moments(prev)
                if s.n0 > NG and s.g == 1 and kt == 2:
                    router_norm(prev, False)
                for at, name in plan(s.n0):
                    if at == kt:
                        unit(s, name)

            def step(s):
                chunks = row_max_chunks(s.n0)
                for kt in range(KT):
                    for i in range(5 * kt, min(5 * kt + 5, len(chunks))):
                        if i == 5 * kt + 4:
                            between(s, kt, i)
                        ahead, t, h, c = chunks[i]
                        row_max(s.after(ahead), t, h, c)
                        if (t, h, c) == (QT - 1, HG - 1, 3):
                            neg_max(s.after(ahead))
                    if 5 * kt + 4 >= len(chunks):
                        between(s, kt, len(chunks))

            for what, i in PROLOGUE_DVE:
                if what == "xt":
                    x_normal(i)
                else:
                    q, h = i
                    for c in range(4):
                        row_max(Step(q // QT), q % QT, h, c)
                    if i == (QT - 1, HG - 1):
                        neg_max(Step(0))
            neg_to_parts(Step(0))
            dve.wait_ge(mlp_in, 16 * 8)
            dve.wait_ge(gates_ready, 1)
            dve.tensor_scalar(b2_sb[:, :], b2_sb[:, :], gate[:, 0:1], None, ALU.mult).then_inc(b2_scaled, 1)
            run_steps(dve, step)

            last, past = Step(STEPS - 1), Step(STEPS)
            denominators(last)
            for _, name in MLP_UNITS:
                unit(past, name)
            router_moments(last)
            router_norm(last, False)

            dve.wait_ge(offs_ready, 1)
            dve.tensor_scalar(part_and[:, :], part_no[:, :], 7, None, ALU.bitwise_and).then_inc(offs_ready, 1)
            dve.wait_ge(offs_ready, 2)
            dve.tensor_scalar(chunk_off, part_and[:, :], 256.0, None, ALU.mult).then_inc(offs_ready, 1)
            dve.tensor_scalar(exp_off, part_no[0:EX, :], float(8 * TOP), None, ALU.mult).then_inc(offs_ready, 1)
            dve.wait_ge(chunk_in, 16)
            n = 0
            for k in range(TOP // 8):
                top8 = cand[:, 8 * k:8 * k + 8]
                if n:
                    dve.wait_ge(cand_ready, n)
                dve.max(top8, chunk_logits).then_inc(cand_ready, 1)
                dve.wait_ge(cand_ready, n + 1)
                dve.max_index(cand_pos[:, 8 * k:8 * k + 8], top8, chunk_logits).then_inc(cand_ready, 1)
                dve.wait_ge(cand_ready, n + 2)
                dve.match_replace(chunk_logits, top8, chunk_logits, -3e38).then_inc(cand_ready, 1)
                n += 3
            dve.wait_ge(cand_ready, n)
            dve.wait_ge(offs_ready, 4)
            dve.tensor_scalar(cand_id, cand_pos, chunk_off, None, ALU.add).then_inc(cand_ready, 1)
            dve.wait_ge(cand_e_in, 16)
            n = 0
            for k in range(TOP // 8):
                top8 = top_v[:, 8 * k:8 * k + 8]
                if n:
                    dve.wait_ge(top_step, n)
                dve.max(top8, cand_e).then_inc(top_step, 1)
                dve.wait_ge(top_step, n + 1)
                if k == 0:
                    dve.tensor_scalar(neg_top, top_v[:, 0:1], -1.0, None, ALU.mult).then_inc(negtop_ready, 1)
                dve.max_index(top_pos[:, 8 * k:8 * k + 8], top8, cand_e).then_inc(top_step, 1)
                dve.wait_ge(top_step, n + 2)
                dve.match_replace(cand_e, top8, cand_e, -3e38).then_inc(top_step, 1)
                n += 3
            dve.wait_ge(top_step, n)
            dve.tensor_scalar(place_id[:, :], top_pos[:, :], exp_off, None, ALU.add).then_inc(place_ready, 1)
            dve.wait_ge(sum_ready, 1)
            dve.reciprocal(exp_rsum, exp_sum).then_inc(weight_ready, 1)
            dve.wait_ge(weight_ready, 1)
            dve.wait_ge(top_exp, 1)
            dve.tensor_scalar(weight[:, :], weight[:, :], exp_rsum, gate[0:EX, 1:2], ALU.mult, ALU.mult
                              ).then_inc(weight_ready, 1)
            for g in range(2):
                for l in range(3):
                    for a4 in range(HALF):
                        a = g * HALF + a4
                        q = (g * 3 + l) * HALF + a4
                        dve.wait_ge(t_filled, q + 1)
                        if q == 0:
                            dve.wait_ge(sum_ready, 1)
                        dve.tensor_copy(h_in[:, a, :, :], ps_t[a4][:, 0:2 * 128]
                                        .rearrange("p (k n) -> p k n", k=2)).then_inc(t_free, 1)
                for a4 in range(HALF):
                    a = g * HALF + a4
                    q = (g * 3 + 2) * HALF + a4
                    dve.wait_ge(l_filled, q + 1)
                    if q == 2 * HALF:
                        dve.wait_ge(weight_in, 16)
                    dve.tensor_scalar(y_out[:, a, :], ps_l[a4][:, 0:D], eb_sb[:, 2, a:a + 1],
                                      weight_slot[:, a:a + 1], ALU.add, ALU.mult).then_inc(l_free, 1)

        @block.tensor
        def _(pe):
            def project(c):
                kind, m, c0, n = PROJ[c]
                if c >= RING:
                    pe.wait_ge(proj_free, c - RING + 1)
                w, src = (wk_sb, ctx_sb) if kind == "k" else (wq_sb, xn_tv)
                rows = CH if kind == "k" else 128
                if kind == "q":
                    pe.wait_ge(xt_free, 2 * (c0 // QB) + 2)
                for k in range(2):
                    last = pe.matmul(ps_s[:, c % RING, 0:n], w[0:rows, k, m * 128:(m + 1) * 128],
                                     src[0:rows, k, c0:c0 + n], start=k == 0, stop=k == 1)
                last.then_inc(proj_filled, 1)

            def transpose_x(b):
                pe.wait_ge(ln_out, QT * (b + 1))
                for k in range(2):
                    if b:
                        pe.wait_ge(xt_free, 2 * b + k - 1)
                    for t in range(QT):
                        last = pe.transpose((ps_m if k == 0 else ps_v)[:, t * 128:(t + 1) * 128],
                                            xn2[:, t, k * 128:(k + 1) * 128], ident[:, :])
                    last.then_inc(xt_filled, 1)

            def values(v):
                keys = 128 if v < KT - 1 else KLAST
                pe.wait_ge(proj_free, NPROJ + v - RING + 1)
                for k in range(2):
                    rows = CH + k
                    last = pe.matmul(ps_s[0:keys, (NPROJ + v) % RING, 0:D], ctx_sb[0:rows, k, v * 128:v * 128 + keys],
                                     wv_sb[0:rows, k, :], start=k == 0, stop=k == 1)
                last.then_inc(proj_filled, 1)

            def row_max(s, t, h, c):
                g_local = (t * HG + h) * 4 + c
                if g_local == 0:
                    wait(pe, q_loaded[s.g], s.block(1, 16))
                    if s.n0 < NG:
                        pe.wait_ge(k_relaid[s.n0], 3 * 16)
                if s.n0 or g_local >= RING:
                    wait(pe, a_free, s.count(ACH, ring_wait(g_local, ACH)))
                c0, n = CHUNKS[c]
                pe.matmul(ps_a[:, g_local % RING, 0:n], q_rows[s.g][0:PARTS, h, t * 128:(t + 1) * 128],
                          k_rows[s.g][0:PARTS, h, c0:c0 + n], start=True, stop=True).then_inc(a_filled, 1)

            def transpose_neg(s):
                wait(pe, neg_ready, s.count(1, 1))
                if s.n0:
                    wait(pe, spare_free, s.use("neg"))
                else:
                    pe.wait_ge(xt_free, 2 * NB)
                pe.transpose(ps_m[0:HG * QT, 0:128], negmax[:, s.g % 2, :], ident[:, :]).then_inc(spare_filled, 1)

            def unit(s, name):
                b = Step(s.n0 - NG, s.r)
                ps_m = bank(s, name)
                if name == "neg":
                    return transpose_neg(s.after(1))
                wait(pe, spare_free, b.use(name if s.n0 < STEPS else first_of(name)))
                if name.startswith("bc"):
                    if name == "bc0":
                        wait(pe, rden_ready, b.block(1))
                    last = pe.matmul(ps_m[:, :], spread[:, int(name[2]), :], rden[:, :], start=True, stop=True)
                elif name.startswith("w1_"):
                    m = int(name[3])
                    for k in range(2):
                        last = pe.matmul(ps_m[:, :], w1_sb[:, k, m * 128:(m + 1) * 128], att_t[:, k, :],
                                         start=k == 0, stop=k == 1)
                elif name.startswith("w2_"):
                    t = int(name[3])
                    for k in range(4):
                        last = pe.matmul(ps_m[:, 0:D], hidden[:, k, t * 128:(t + 1) * 128], w2_sb[:, k, :],
                                         start=k == 0, stop=k == 3)
                elif name.startswith("tr"):
                    k = int(name[2])
                    wait(pe, ln_out, b.block(1, QT) + NB * QT)
                    for t in range(QT):
                        last = pe.transpose(ps_m[:, t * 128:(t + 1) * 128], xn2[:, t, k * 128:(k + 1) * 128],
                                            ident[:, :])
                elif name == "lg":
                    for k in range(2):
                        last = pe.matmul(ps_m[0:EX, :], wg_sb[:, k, :], xn2_t[:, k, :], start=k == 0, stop=k == 1)
                last.then_inc(spare_filled, 1)

            def times_v(s, kt):
                keys = 128 if kt < KT - 1 else KLAST
                wait(pe, exp_done, s.count(TILES, HG * (kt + 1)))
                if kt == 0 and s.n0:
                    wait(pe, pv_out, s.count(1))
                for h in range(HG):
                    last = pe.matmul(ps_v[32 * h:32 * h + DH + 1, :], v_cols[s.g][0:keys, kt, h, :],
                                     probs[0:keys, (s.g * KT + kt) % 2, h, :], start=kt == 0, stop=kt == KT - 1)
                last.then_inc(pv_done, 1)

            def step(s):
                chunks = row_max_chunks(s.n0)
                todo = iter(chunks)

                def next_chunk():
                    for ahead, t, h, c in todo:
                        row_max(s.after(ahead), t, h, c)
                        break

                for kt in range(KT):
                    keys = 128 if kt < KT - 1 else KLAST
                    for h in range(HG):
                        j = HG * kt + h
                        if s.n0 * TILES + j >= RING:
                            wait(pe, exp_done, s.count(TILES, ring_wait(j, TILES)))
                        if kt == 0 and h == 0:
                            wait(pe, neg_rows, s.count(NEG_DMAS, NEG_DMAS))
                        pe.matmul(ps_s[0:keys, j % RING, :], k_rows[s.g][0:PARTS + 3, h, kt * 128:kt * 128 + keys],
                                  q_rows[s.g][0:PARTS + 3, h, :], start=True, stop=True).then_inc(scores_ready, 1)
                        next_chunk()
                    if kt:
                        times_v(s, kt - 1)
                    elif s.n0:
                        times_v(s.after(-1), KT - 1)
                    for at, name in plan(s.n0):
                        if at == kt:
                            unit(s, name)
                    next_chunk()

            pe.wait_ge(ctx_in, 64)
            pe.wait_ge(ident_in, 16)
            for what, i in PROLOGUE:
                if what == "proj":
                    if PROJ[i][0] == "q":
                        pe.wait_ge(q_in, 16)
                    project(i)
                elif what == "xt":
                    transpose_x(i)
                elif what == "v":
                    if i == 0:
                        pe.wait_ge(v_in, 48)
                    values(i)
                else:
                    q, h = i
                    for c in range(4):
                        row_max(Step(q // QT), q % QT, h, c)
            transpose_neg(Step(0))
            pe.wait_ge(proj_free, NPROJ + KT)
            pe.wait_ge(ones_in, 16 * NG)
            pe.wait_ge(mlp_in, 16 * 8)
            run_steps(pe, step)

            last, past = Step(STEPS - 1), Step(STEPS)
            times_v(last, KT - 1)
            for _, name in MLP_UNITS + LN_UNITS:
                unit(past, name)

            pe.wait_ge(spare_free, len(ORDER))
            for g in range(2):
                for l in range(3):
                    for a4 in range(HALF):
                        a = g * HALF + a4
                        q = (g * 3 + l) * HALF + a4
                        if l == 0:
                            pe.wait_ge(x_gathered[a], 16)
                            src = tok_x[:, a, :]
                            if q >= HALF:
                                pe.wait_ge(t_free, q - HALF + 1)
                        else:
                            pe.wait_ge(l_free, q - HALF + 1)
                            src = h_out[:, a, :]
                        for k in range(2):
                            last = pe.transpose(ps_t[a4][:, k * 128:(k + 1) * 128],
                                                src[:, k * 128:(k + 1) * 128], ident[:, :])
                        last.then_inc(t_filled, 1)
                    for a4 in range(HALF):
                        a = g * HALF + a4
                        q = (g * 3 + l) * HALF + a4
                        if a4 == 0 and g == 0:
                            pe.wait_ge(w_in[l], 16 * expert_dmas(l))
                        pe.wait_ge(t_free, q + 1)
                        if q >= HALF:
                            pe.wait_ge(l_free, q - HALF + 1)
                        for k in range(2):
                            for e2 in range(2):
                                last = pe.matmul(ps_l[a4][e2 * TOP:(e2 + 1) * TOP, 0:D],
                                                 h_in[:, a, k, e2 * TOP:(e2 + 1) * TOP],
                                                 w_exp[:, l, 2 * a + e2, k, :], start=k == 0, stop=k == 1)
                        last.then_inc(l_filled, 1)


def prologue_order():
    order = [("proj", c) for c in range(4)] + [("xt", 0), ("proj", 4)] + [("proj", c) for c in range(5, 9)]
    rest = [("proj", 9), ("xt", 1), ("proj", 10), ("proj", 11), ("xt", 2), ("proj", 12), ("proj", 13),
            ("xt", 3), ("proj", 14), ("proj", 15)] + [("v", v) for v in range(KT)]
    for q in range(QT + LEAD):
        for h in range(HG):
            order.append(("max", (q, h)))
            order += rest[:2] if len(rest) > 4 * (QT + LEAD) - (q * HG + h) else rest[:1]
            rest = rest[2:] if len(rest) > 4 * (QT + LEAD) - (q * HG + h) else rest[1:]
    return order + rest


def prologue_order_dve():
    order = [u for u in PROLOGUE if u[0] == "max" or u[0] == "xt" and u[1]]
    for b in range(1, NB):
        at = order.index(("xt", b))
        order[at - 1:at + 1] = [order[at], order[at - 1]]
    return order


PROLOGUE = prologue_order()
PROLOGUE_DVE = prologue_order_dve()


def kernel(x, ctx_768, g_xattn, g_ffn, L0_xattn_Wq, L0_xattn_bq, L0_xattn_Wk, L0_xattn_bk, L0_xattn_Wv,
           L0_xattn_bv, L0_xattn_W1, L0_xattn_b1, L0_xattn_W2, L0_xattn_b2, L0_ffn_Wg, L0_ffn_bg, L0_ffn_w1,
           L0_ffn_b1, L0_ffn_w2, L0_ffn_b2, L0_ffn_w3, L0_ffn_b3):
    import ml_dtypes
    import numpy as np
    import concourse.bacc as bacc
    from concourse.bass_utils import run_bass_kernel_spmd

    def d_major(a):
        a = np.asarray(a)
        return a.reshape(-1, 2, HM, DH).transpose(0, 1, 3, 2).reshape(-1, D)

    def rows(a, k):
        return np.asarray(a).reshape(k, 128).T

    head_of_row = np.arange(D).reshape(2, 128) // DH
    arrays = {
        "ident": np.eye(128, dtype=np.float32),
        "spread": (np.arange(128)[:, None, None] == head_of_row).astype(np.float32),
        "ones": np.ones((3, HG * S), ml_dtypes.bfloat16),
        "ones_row": np.ones((1, S), np.float32),
        "x": np.asarray(x)[0],
        "ctx_t": np.asarray(ctx_768)[0].T,
        "wq": d_major(L0_xattn_Wq),
        "bqk": np.stack([rows(d_major(L0_xattn_bq), 2), rows(d_major(L0_xattn_bk), 2)], axis=1),
        "wk": d_major(L0_xattn_Wk),
        "wv": np.asarray(L0_xattn_Wv),
        "bv": np.asarray(L0_xattn_bv).reshape(1, D),
        "w1": np.asarray(L0_xattn_W1),
        "b1": rows(L0_xattn_b1, 4),
        "w2": np.asarray(L0_xattn_W2),
        "b2": np.broadcast_to(np.asarray(L0_xattn_b2), (128, D)),
        "wg": np.asarray(L0_ffn_Wg),
        "bg": np.asarray(L0_ffn_bg).reshape(EX, 1),
        "gates": np.broadcast_to(np.concatenate([np.asarray(g_xattn), np.asarray(g_ffn)]), (128, 2)),
        "ew1": np.asarray(L0_ffn_w1),
        "ew2": np.asarray(L0_ffn_w2),
        "ew3": np.asarray(L0_ffn_w3),
        "eb": np.stack([np.repeat(np.asarray(b).reshape(EX // 2, 2).T, TOP, axis=0)
                        for b in (L0_ffn_b1, L0_ffn_b2, L0_ffn_b3)], axis=1),
    }
    arrays = {k: np.ascontiguousarray(v) for k, v in arrays.items()}
    nc = bacc.Bacc("TRN2", target_bir_lowering=False, num_devices=1)
    ap = {k: nc.dram_tensor("in_" + k, v.shape, mybir.dt.from_np(v.dtype), kind="ExternalInput").ap()
          for k, v in arrays.items()}
    out = nc.dram_tensor("out", (1, T, D), F32, kind="ExternalOutput").ap()
    flamingo(nc, ap["ident"], ap["spread"], ap["ones"], ap["ones_row"], ap["x"], ap["ctx_t"], ap["wq"], ap["bqk"], ap["wk"], ap["wv"], ap["bv"], ap["w1"], ap["b1"],
             ap["w2"], ap["b2"], ap["wg"], ap["bg"], ap["gates"], (ap["ew1"], ap["ew2"], ap["ew3"]), ap["eb"],
             out.rearrange("o t d -> (o t) d"))
    result = run_bass_kernel_spmd(nc, [{"in_" + k: v for k, v in arrays.items()}], core_ids=[0])
    return result.results[0]["out"]
```

```python
import concourse.bass as bass
from concourse import mybir
from contextlib import ExitStack

F32, BF16, U32, I32 = mybir.dt.float32, mybir.dt.bfloat16, mybir.dt.uint32, mybir.dt.int32
ALU, ACT, AX = mybir.AluOpType, mybir.ActivationFunctionType, mybir.AxisListType

T, D, C, S = 2048, 256, 192, 1601
H, DH = 16, 16
FF = 2 * D
EX, TOP = 16, 64
EPS = 1e-5
SCALE = 1.0 / DH ** 0.5

QB = 512
NB = T // QB
HG = 4
NG = H // HG
STEPS = NB * NG
QT = QB // 128
KT = -(-S // 128)
KLAST = S - (KT - 1) * 128
TILES = HG * KT
RING = 3
KC = -(-S // 4)
CHUNKS = [(c * KC, min(KC, S - c * KC)) for c in range(4)]
QCHUNKS = HG * 4
ACH = QT * QCHUNKS
LEAD = 1
PARTS = 3 * DH * 2
LATE_LOADS = 10
HM = 8
CH = C // 2

K_WORDS, Q_WORDS, V_WORDS = HG * S // 2, HG * QB // 2, KT * HG * (DH + 1)
GROUP_WORDS = K_WORDS + Q_WORDS + V_WORDS
EXPERT_WORDS = 2 * D
FIT = [0, 0, 2 * GROUP_WORDS // EXPERT_WORDS, 3 * GROUP_WORDS // EXPERT_WORDS, 3 * EX]

PROJ = ([("k", 0, c, n) for c, n in CHUNKS] + [("k", 1, *CHUNKS[0]), ("q", 0, 0, QB)]
        + [("k", 1, c, n) for c, n in CHUNKS[1:]] + [("q", 1, 0, QB)] + [("q", m, b * QB, QB) for b in range(1, NB) for m in (0, 1)])
NPROJ = len(PROJ)
ON_GPSIMD = [4] + list(range(6, NPROJ))
ON_VECTOR = [c for c in range(NPROJ) if c not in ON_GPSIMD]
SPLIT_BUFS = 6
SPREAD = 0.85

MLP_UNITS = [(4, "bc0"), (5, "bc1"), (6, "w1_0"), (7, "w1_1"), (8, "w1_2"), (9, "w1_3"), (11, "w2_0"), (12, "w2_1")]
LN_UNITS = [(5, "tr0"), (6, "tr1"), (8, "lg")]
NEG_AT = 10
TILE_CHUNKS = [HG + 1] * (KT - 1) + [HG]
FIRST_CHUNK = [sum(TILE_CHUNKS[:kt]) for kt in range(KT + 1)]


TC = 256
NC = (T - QB) // TC
LAST0 = EX * TOP


def offsets():
    p = list(range(128))
    return ([TC * (i % NC) for i in p], [TOP * NC * i for i in p],
            [i % 2 * TOP * EX // 2 + i // 2 - (LAST0 - TOP) for i in p])


PAIRS = EX // 2
GROUPS = [(0, 1, 2), (3, 4, 5), (6, 7)]
ITEMS = [(a, l) for pairs in GROUPS for l in range(3) for a in pairs]
RELUS = [it for it in ITEMS if it[1] < 2]
OUTS = [it for it in ITEMS if it[1] == 2]


def plan(n):
    units = []
    if n >= NG:
        units += MLP_UNITS if n % NG == 0 else LN_UNITS if n % NG == 1 else []
    if n < STEPS - 1:
        units = units + [(NEG_AT, "neg")]
    return sorted(units, key=lambda u: u[0])


def spare_bank_order():
    order = [("neg", 0)]
    for n in range(STEPS):
        order += [("neg", n + 1) if u == "neg" else (u, n // NG - 1) for _, u in plan(n)]
    order += [(u, NB - 1) for _, u in MLP_UNITS + LN_UNITS]
    return {key: k for k, key in enumerate(order)}


ORDER = spare_bank_order()
USES_PER_BLOCK = NG + len(MLP_UNITS) + len(LN_UNITS)


def expert_dmas(layer):
    cuts = sorted({4 * k for k in range(3 * EX // 4)} | {f for f in FIT if f < 3 * EX})
    return sum(layer * EX <= c < (layer + 1) * EX for c in cuts)


def ring_bank(j, per_step):
    return 1 if j == per_step - 1 else j % RING


def ring_wait(j, per_step):
    bank = ring_bank(j, per_step)
    before = [k for k in range(j) if ring_bank(k, per_step) == bank]
    if before:
        return before[-1] + 1
    return max(k for k in range(per_step) if ring_bank(k, per_step) == bank) + 1 - per_step


class Step:

    def __init__(self, n0, r=None):
        self.n0, self.r, self.g = n0, r, n0 % NG

    def after(self, k):
        return Step(self.n0 + k, self.r)

    def count(self, per_step, plus=0):
        const = per_step * self.n0 + plus
        return const if self.r is None else self.r * (per_step * NG) + const

    def use(self, unit):
        k = ORDER[(unit, self.n0 if unit == "neg" else self.n0 // NG)]
        return k if self.r is None else self.r * USES_PER_BLOCK + k

    def block(self, plus=0, scale=1):
        const = (self.n0 // NG + plus) * scale
        return const if self.r is None else self.r * scale + const

    def halves(self, scale):
        const = self.n0 // 2 * scale
        return const if self.r is None else self.r * (NG // 2 * scale) + const


def wait(eng, sem, value):
    if not isinstance(value, int) or value > 0:
        eng.wait_ge(sem, value)


def run_steps(eng, step):
    for n in (0, 1):
        step(Step(n))
    with eng.Fori(0, NB - 1) as r:
        for n in range(2, 2 + NG):
            step(Step(n, r))
    for n in (STEPS - 2, STEPS - 1):
        step(Step(n))


def row_max_chunks(n0):
    out = []
    for q in range(QT):
        ahead, t = 1 + (q + LEAD) // QT, (q + LEAD) % QT
        if n0 + ahead < STEPS:
            out += [(ahead, t, h, c) for h in range(HG) for c in range(4)]
    return out


def flamingo(nc, const, x, ctx_t, wq, b_qk, wk, wv, bv, w1, b1, w2, b2, wg, bg, gates, ew, eb, out):
    es = ExitStack()
    with es:
        def sb(name, shape, dt):
            return es.enter_context(nc.sbuf_tensor(name, shape, dt))

        def pb(name, shape, dt):
            return es.enter_context(nc.psum_tensor(name, shape, dt))

        def sem(name):
            return es.enter_context(nc.semaphore(name))

        def dram(name, shape, dt):
            return nc.dram_tensor(name, shape, dt, kind="Internal").ap()

        region = sb("region", [128, 3 * EX * 2 * D], F32)
        k_rows, q_rows, v_cols = [], [], []
        for g in range(NG):
            at = g * GROUP_WORDS
            k_rows.append(region[:, at:at + K_WORDS].bitcast(BF16).rearrange("p (h s) -> p h s", h=HG))
            at += K_WORDS
            q_rows.append(region[:, at:at + Q_WORDS].bitcast(BF16).rearrange("p (h n) -> p h n", h=HG))
            at += Q_WORDS
            v_cols.append(region[:, at:at + V_WORDS].rearrange("p (k h d) -> p k h d", k=KT, h=HG))
        p_flat = region[:, NG * GROUP_WORDS:NG * GROUP_WORDS + 2 * HG * QB]
        probs = p_flat.rearrange("p (s h n) -> p s h n", s=2, h=HG)
        w_exp = region[:, :].rearrange("p (l e k o) -> p l e k o", l=3, e=EX, k=2)

        x_in = sb("x_in", [128, T // 128, D], F32)
        xn_t = sb("xn_t", [128, 2 * T], F32)
        xn_tv = xn_t[:, :].rearrange("p (k n) -> p k n", k=2)
        hidden = xn_t[:, 0:4 * QB].rearrange("p (m n) -> p m n", m=4)
        att_t = xn_t[:, 4 * QB:6 * QB].rearrange("p (k n) -> p k n", k=2)
        xn2_t = xn_t[:, 6 * QB:8 * QB].rearrange("p (k n) -> p k n", k=2)
        ctx_sb = sb("ctx_sb", [128, 2, S], F32)
        logits = ctx_sb[0:EX, :, :].rearrange("p k s -> p (k s)")[:, 0:T]
        wq_sb = sb("wq_sb", [128, 2, D], F32)
        wk_sb = sb("wk_sb", [CH, 2, D], F32)
        wv_sb = sb("wv_sb", [CH + 1, 2, D], F32)
        bqk = sb("bqk", [128, 2, 2], F32)
        w1_sb = sb("w1_sb", [128, 2, FF], F32)
        b1_sb = sb("b1_sb", [128, 4], F32)
        w2_sb = sb("w2_sb", [128, 4, D], F32)
        b2_sb = sb("b2_sb", [128, D], F32)
        wg_sb = sb("wg_sb", [128, 2, EX], F32)
        bg_sb = sb("bg_sb", [EX, 1], F32)
        eb_sb = sb("eb_sb", [128, 3, EX // 2], F32)
        gate_in = sb("gate_in", [128, 2], F32)
        gate = sb("gate", [128, 2], F32)
        eps = sb("eps", [128, 1], F32)
        ident = sb("ident", [128, 128], F32)
        spread = sb("spread", [128, 2, 128], F32)
        stats = sb("stats", [128, T // 128, 6], F32)
        moments = sb("moments", [128, T // 128, 2], F32)
        std = sb("std", [128, T // 128], F32)
        carrier = sb("carrier", [128, 3], F32)
        rstd = sb("rstd", [128, T // 128], F32)
        x2 = sb("x2", [128, QT, D], F32)
        xn2 = sb("xn2", [128, QT, D], F32)
        att_raw = sb("att_raw", [128, 2, QB], F32)
        den = sb("den", [128, H * QB // 128], F32)
        den_inv = sb("den_inv", [128, H * QB // 128], F32)
        rden = sb("rden", [128, QB], F32)
        pv_raw = sb("pv_raw", [128, 2, QB], F32)
        cmax = sb("cmax", [128, 2, HG * QT * 4], F32)
        negmax = sb("negmax", [128, 2, HG * QT], F32)
        neg_parts = sb("neg_parts", [HG * QT, 3, 128], BF16)
        neg_rest = sb("neg_rest", [HG * QT, 128], F32)
        cand_space = sb("cand_space", [128, 1024], F32)
        split_own = sb("split_own", [128, 2, 7 * QB // 2], F32)

        def three_parts(buf):
            return buf.bitcast(BF16).rearrange("p (j n) -> p j n", j=3)

        SPLIT = [(buf[:, 0:QB], buf[:, QB:2 * QB], three_parts(buf[:, 2 * QB:7 * QB // 2]))
                 for buf in (p_flat[:, 0:4 * QB], p_flat[:, 4 * QB:8 * QB], split_own[:, 0, :], split_own[:, 1, :])]
        x2_flat, pv_flat = (b[:, :, :].rearrange("p a n -> p (a n)") for b in (x2, pv_raw))
        SPLIT += [(att_raw[:, 0, :], att_raw[:, 1, :], three_parts(pv_flat[:, 0:3 * QB // 2])),
                  (x2_flat[:, 0:QB], x2_flat[:, QB:2 * QB], three_parts(cand_space[:, 0:3 * QB // 2]))]

        q_scr = [dram(f"q_scr{m}", [3, 128, T], BF16) for m in range(2)]
        k_scr = [dram(f"k_scr{m}", [3, 128, S], BF16) for m in range(2)]
        xn2_scr = dram("xn2_scr", [T - QB, D], F32)
        logit_scr = dram("logit_scr", [EX, T - QB], F32)
        cand_scr = dram("cand_scr", [EX * NC, TOP], F32)
        cand_id_scr = dram("cand_id_scr", [EX * NC * TOP, 1], U32)
        id_table = dram("id_table", [LAST0 + QB, 1], U32)
        row_table = dram("row_table", [LAST0 + QB, D], F32)
        odd_sum = dram("odd_sum", [T, D], F32)

        ps_s = pb("ps_s", [128, RING, 512], F32)
        ps_a = pb("ps_a", [128, RING, 512], F32)
        ps_v = pb("ps_v", [128, 512], F32)
        ps_m = pb("ps_m", [128, 512], F32)

        ctx_in, q_in, v_in, mlp_in = sem("ctx_in"), sem("q_in"), sem("v_in"), sem("mlp_in")
        x_loaded = [sem(f"x_loaded{b}") for b in range(NB)]
        gates_in, gates_ready = sem("gates_in"), sem("gates_ready")
        eps_ready, ident_in, ones_in, v_ones, rden_zero = (
            sem("eps_ready"), sem("ident_in"), sem("ones_in"), sem("v_ones"), sem("rden_zero"))
        b2_scaled, x_biased = sem("b2_scaled"), sem("x_biased")
        ln_stat, ln_mean, ln_std, ln_rstd, ln_out = (
            sem("ln_stat"), sem("ln_mean"), sem("ln_std"), sem("ln_rstd"), sem("ln_out"))
        xt_filled, xt_free = sem("xt_filled"), sem("xt_free")
        proj_filled, proj_free, part1_ready = sem("proj_filled"), sem("proj_free"), sem("part1_ready")
        part2_ready = sem("part2_ready")
        split_v, split_g = sem("split_v"), sem("split_g")
        stored = [sem(f"stored{c}") for c in range(NPROJ)]
        k_relaid = [sem(f"k_relaid{g}") for g in range(NG)]
        q_loaded = [sem(f"q_loaded{g}") for g in range(NG)]
        a_filled, a_free, neg_ready = sem("a_filled"), sem("a_free"), sem("neg_ready")
        spare_filled, spare_free = sem("spare_filled"), sem("spare_free")
        neg_split, neg_rows = sem("neg_split"), sem("neg_rows")
        scores_ready, exp_done, pv_done, pv_out = (
            sem("scores_ready"), sem("exp_done"), sem("pv_done"), sem("pv_out"))
        att_moved, rden_ready = [sem(f"att_moved{i}") for i in range(2)], sem("rden_ready")
        den_moved, den_inverted = [sem(f"den_moved{i}") for i in range(2)], sem("den_inverted")
        logit_stored = sem("logit_stored")
        x2_free, xn2_free = sem("x2_free"), sem("xn2_free")

        chunk_logits = cand_space[0:EX * NC, 0:TC]
        cand = cand_space[0:EX * NC, TC:TC + TOP]
        cand_pos = cand_space[0:EX * NC, TC + TOP:TC + 2 * TOP].bitcast(U32)
        cand_id = cand_space[0:EX * NC, TC + 2 * TOP:TC + 3 * TOP].bitcast(U32)
        cand_e = cand_space[0:EX, TC + 3 * TOP:TC + (3 + NC) * TOP]
        finalists = sb("finalists", [EX, TOP + QB], F32)
        early_pos = sb("early_pos", [EX, TOP], U32)
        top_v = sb("top_v", [EX, TOP], F32)
        top_pos = sb("top_pos", [EX, TOP], U32)
        place = sb("place", [EX, TOP], F32)
        place_tmp = sb("place_tmp", [EX, 2, TOP], F32)
        weight = sb("weight", [EX, TOP], F32)
        small = sb("small", [128, 8], F32)
        off = sb("off", [128, 3], F32)
        place_slot = sb("place_slot", [128, EX // 2], U32)
        weight_slot = sb("weight_slot", [128, EX // 2], F32)
        token_slot = sb("token_slot", [128, EX // 2], U32)
        token_f = sb("token_f", [128, PAIRS], F32)
        token_odd = sb("token_odd", [TOP, PAIRS], U32)
        zeros = sb("zeros", [128, D], F32)
        tok_x = x_in[:, 0:EX // 2, :]
        h_in = xn_t[:, 0:8 * D].rearrange("p (a k n) -> p a k n", a=EX // 2, k=2)
        h_out = xn_t[:, 8 * D:16 * D].rearrange("p (a n) -> p a n", a=EX // 2)
        y_out = x_in[:, EX // 2:EX, :]
        w_in = [sem(f"w_in{l}") for l in range(3)]
        chunk_in, cand_ready, cand_stored, cand_id_stored, cand_e_in = (
            sem("chunk_in"), sem("cand_ready"), sem("cand_stored"), sem("cand_id_stored"), sem("cand_e_in"))
        early_step, early_stored, top_step = sem("early_step"), sem("early_stored"), sem("top_step")
        place_ready, slots_filled, place_in = sem("place_ready"), sem("slots_filled"), sem("place_in")
        sum_ready, weight_ready, weight_in = sem("sum_ready"), sem("weight_ready"), sem("weight_in")
        negtop_ready, top_exp, last_logits = sem("negtop_ready"), sem("top_exp"), sem("last_logits")
        token_in = [sem(f"token_in{a}") for a in range(EX // 2)]
        token_f_ready, odd_filled, odd_ready = sem("token_f_ready"), sem("odd_filled"), sem("odd_ready")
        zeros_ready, odd_zero = sem("zeros_ready"), sem("odd_zero")
        x_gathered = [sem(f"x_gathered{a}") for a in range(EX // 2)]
        t_filled, t_free, l_filled = sem("t_filled"), sem("t_free"), sem("l_filled")
        relu_done, y_ready = sem("relu_done"), sem("y_ready")
        scattered = [sem(f"scattered{h}") for h in range(2)]
        merged = sem("merged")
        neg_top = small[0:EX, 2:3]
        exp_sum = small[0:EX, 3:4]
        exp_rsum = small[0:EX, 4:5]
        slots = ps_a[:, 2, 0:EX]
        ps_t = [ps_a[:, 0, :], ps_a[:, 1, :], ps_v[:, :]]
        ps_l = [ps_s[:, i, :] for i in range(3)]
        tail_banks = [ps_m[:, :], ps_a[:, 0, :], ps_a[:, 1, :], ps_a[:, 2, :]]

        block = es.enter_context(nc.Block())

        def part(c, j, n):
            return SPLIT[c % SPLIT_BUFS][2][:, 2 - j if PROJ[c][0] == "k" else j, 0:n]

        NEG_DMAS, ATT_DMAS = 3 * 16, HG * 16

        def bank(s, name):
            return ps_m[:, :] if s.n0 < STEPS else tail_banks[int(name[-1]) if name != "lg" else 0]

        def score_bank(s, j):
            if s.n0 < STEPS - 1:
                return ps_s[:, ring_bank(j, TILES), :]
            return (ps_s if j % (2 * RING) < RING else ps_a)[:, j % RING, :]

        def first_of(name):
            return name[:-1] + "0" if name != "lg" else name

        @block.sync
        def _(sp):
            for k in range(2):
                sp.dma_start(ctx_sb[0:CH, k, :], ctx_t[k * CH:(k + 1) * CH, :]).then_inc(ctx_in, 16)
                if k == 0:
                    sp.dma_start(wk_sb[:, :, :], wk.rearrange("(k p) o -> p k o", k=2)).then_inc(ctx_in, 16)

            def load_x(b):
                sp.dma_start(x_in[:, b * QT:(b + 1) * QT, :],
                             x[b * QB:(b + 1) * QB, :].rearrange("(t p) d -> p t d", p=128)
                             ).then_inc(x_loaded[b], 16)

            load_x(0)
            sp.dma_start(ident[:, :], const["ident"]).then_inc(ident_in, 16)
            sp.dma_start(gate_in[:, :], gates).then_inc(gates_in, 16)
            sp.dma_start(bqk[:, :, :], b_qk).then_inc(ctx_in, 16)
            sp.dma_start(wq_sb[:, :, :], wq.rearrange("(k p) o -> p k o", k=2)).then_inc(q_in, 16)
            for b in range(1, NB):
                load_x(b)
            sp.dma_start(wv_sb[0:CH, :, :], wv.rearrange("(k p) o -> p k o", k=2)).then_inc(v_in, 16)
            sp.dma_start(wv_sb[CH:CH + 1, 1, :], bv).then_inc(v_in, 16)
            sp.dma_start(ctx_sb[CH:CH + 1, 1, :], const["ones_row"]).then_inc(v_in, 16)

            def load_ones():
                for g in range(NG):
                    sp.dma_start(k_rows[g][PARTS:PARTS + 3, :, :].rearrange("p h s -> p (h s)"), const["ones"]
                                 ).then_inc(ones_in, 16)

            def load_mlp():
                sp.dma_start(spread[:, :, :], const["spread"]).then_inc(mlp_in, 16)
                sp.dma_start(off[:, :], const["offsets"]).then_inc(mlp_in, 16)
                sp.dma_start(id_table[LAST0:LAST0 + QB, :], const["last_tokens"]).then_inc(mlp_in, 16)
                sp.dma_start(b2_sb[:, :], b2).then_inc(mlp_in, 16)
                sp.dma_start(w1_sb[:, :, :], w1.rearrange("(k p) o -> p k o", k=2)).then_inc(mlp_in, 16)
                sp.dma_start(b1_sb[:, :], b1).then_inc(mlp_in, 16)
                sp.dma_start(w2_sb[:, :, :], w2.rearrange("(k p) o -> p k o", k=4)).then_inc(mlp_in, 16)
                sp.dma_start(wg_sb[:, :, :], wg.rearrange("(k p) o -> p k o", k=2)).then_inc(mlp_in, 16)
                sp.dma_start(bg_sb[:, :], bg).then_inc(mlp_in, 16)
                sp.dma_start(eb_sb[:, :, :], eb).then_inc(mlp_in, 16)

            def store(c):
                kind, m, c0, n = PROJ[c]
                if c in ON_VECTOR:
                    sp.wait_ge(split_v, 3 * (ON_VECTOR.index(c) + 1))
                else:
                    sp.wait_ge(split_g, 2 * (ON_GPSIMD.index(c) + 1))
                sp.dma_start((k_scr if kind == "k" else q_scr)[m][:, :, c0:c0 + n].rearrange("j p n -> p j n"),
                             SPLIT[c % SPLIT_BUFS][2][:, :, 0:n]).then_inc(stored[c], 16)

            def relay_k(g):
                m, h0 = g * HG // HM, g * HG % HM
                for c in range(NPROJ):
                    if PROJ[c][:2] == ("k", m):
                        sp.wait_ge(stored[c], 16)
                for row, parts in ((0, 3), (3, 2), (5, 1)):
                    src = k_scr[m][3 - parts:3, :, :].rearrange("j (d h) n -> (j d) h n", h=HM)
                    sp.dma_start(k_rows[g][row * DH:(row + parts) * DH, :, :],
                                 src[:, h0:h0 + HG, :]).then_inc(k_relaid[g], 16)

            def load_q(s):
                m, h0 = s.g * HG // HM, s.g * HG % HM
                for row, parts in ((0, 3), (3, 2), (5, 1)):
                    src = q_scr[m][0:parts, :, :].rearrange("j (d h) n -> (j d) h n", h=HM)
                    sp.dma_start(q_rows[s.g][row * DH:(row + parts) * DH, :, :],
                                 src[:, h0:h0 + HG, bass.ds(s.block(scale=QB), QB)]).then_inc(q_loaded[s.g], 16)

            def put_neg(s):
                for j in range(3):
                    sp.wait_ge(neg_split, s.count(3, j + 1))
                    sp.dma_start(q_rows[s.g][PARTS + j:PARTS + j + 1, :, :].rearrange("p h n -> p (h n)"),
                                 neg_parts[:, j, :]).then_inc(neg_rows, 16)

            def move_attention(s):
                wait(sp, pv_out, s.count(1, 1))
                if s.g == 0 and s.n0 >= NG:
                    wait(sp, spare_free, Step(s.n0 - NG, s.r).use("bc1") + 1)
                sp.dma_start(den[s.g * 128 // NG:(s.g + 1) * 128 // NG, :],
                             pv_raw[DH:128:32, s.g % 2, :]).then_inc(den_moved[s.g % 2], 16)
                for h in range(HG):
                    r0 = (s.g % 2) * HG * DH + h * DH
                    sp.dma_start(att_raw[r0:r0 + DH, s.g // 2, :],
                                 pv_raw[32 * h:32 * h + DH, s.g % 2, :]).then_inc(att_moved[s.g % 2], 16)

            def move_inverses(b):
                sp.wait_ge(rden_zero, 1)
                wait(sp, den_inverted, b.block(1))
                sp.dma_start(rden[0:H, :], den_inv[:, :]).then_inc(rden_ready, 16)

            def store_x2(b):
                wait(sp, spare_free, b.use("w2_1") + 1)
                sp.dma_start(out[bass.ds(b.block(scale=QB), QB), :].rearrange("(t p) d -> p t d", p=128),
                             x2[:, :, :]).then_inc(x2_free, 16)

            def store_xn2(b):
                wait(sp, ln_out, b.block(1, QT) + NB * QT)
                place = (row_table[LAST0:LAST0 + QB, :] if b.n0 == STEPS - 1 else
                         xn2_scr[bass.ds(b.block(scale=QB), QB), :])
                sp.dma_start(place.rearrange("(t p) d -> p t d", p=128), xn2[:, :, :]).then_inc(xn2_free, 16)

            def store_logits(b):
                wait(sp, spare_free, b.use("lg") + 1)
                sp.dma_start(logit_scr[:, bass.ds(b.block(scale=QB), QB)],
                             logits[:, bass.ds(b.block(scale=QB), QB)]).then_inc(logit_stored, 16)

            for c in range(4):
                store(c)
            relay_k(0)
            store(5)
            load_ones()
            sp.wait_ge(stored[5], 16)
            load_q(Step(0))
            store(4)
            relay_k(1)
            load_q(Step(1))
            load_mlp()
            sp.wait_ge(zeros_ready, 1)
            sp.dma_start(odd_sum.rearrange("(p t) d -> p t d", p=128),
                         zeros[:, :].rearrange("p (o d) -> p o d", o=1).broadcast_to([128, T // 128, D])
                         ).then_inc(odd_zero, 16)
            for c in range(6, 12):
                store(c)
                if c == 9:
                    relay_k(2)
                    relay_k(3)
            put_neg(Step(0))
            for c in range(12, NPROJ):
                store(c)

            def load_experts(groups, upto):
                for u in range(FIT[groups], FIT[upto]):
                    l, e = u // EX, u % EX
                    if u in FIT or e % 4 == 0:
                        n = min([4 - e % 4] + [f - u for f in FIT if f > u])
                        sp.dma_start(w_exp[:, l, e:e + n, :, :].rearrange("p e k o -> p (e k) o"),
                                     ew[l][e:e + n, :, :].rearrange("e (k p) o -> p (e k) o", k=2)
                                     ).then_inc(w_in[l], 16)

            def step(s):
                if s.n0 >= 1:
                    move_attention(s.after(-1))
                if s.n0 == STEPS - 2:
                    sp.wait_ge(logit_stored, 16 * (NB - 1))
                    sp.dma_start(chunk_logits, logit_scr.rearrange("e (c n) -> (e c) n", c=NC)
                                 ).then_inc(chunk_in, 16)
                    load_experts(0, 2)
                if s.n0 == 1:
                    for c in range(9, NPROJ):
                        sp.wait_ge(stored[c], 16)
                prev = Step(s.n0 - NG, s.r)
                if s.n0 > NG and s.g == 1:
                    store_x2(prev)
                if s.n0 + 2 < STEPS:
                    wait(sp, scores_ready, s.count(TILES, -TILES))
                    load_q(s.after(2))
                if s.n0 >= NG and s.g == 0:
                    move_inverses(prev)
                if s.n0 > NG and s.g == 1:
                    store_xn2(prev)
                    store_logits(prev)
                if s.n0 + 1 < STEPS:
                    put_neg(s.after(1))

            run_steps(sp, step)
            last = Step(STEPS - 1)
            sp.wait_ge(cand_ready, 25)
            sp.dma_start(cand_scr, cand).then_inc(cand_stored, 16)
            sp.dma_start(cand_id_scr.rearrange("(p n) o -> p (n o)", n=TOP), cand_id).then_inc(cand_id_stored, 16)
            sp.wait_ge(cand_stored, 16)
            sp.dma_start(cand_e, cand_scr.rearrange("(e c) n -> e (c n)", e=EX)).then_inc(cand_e_in, 16)
            move_attention(last)
            move_inverses(last)
            load_experts(2, 4)
            for a in range(EX // 2):
                sp.wait_ge(token_in[a], 16)
            sp.dma_start(id_table[0:LAST0, :].rearrange("(p a) o -> p (a o)", p=128), token_slot[:, :]
                         ).then_inc(early_stored, 16)
            for a in range(EX // 2):
                sp.wait_ge(x_gathered[a], 16)
            sp.dma_start(row_table[0:LAST0, :].rearrange("(p a) d -> p a d", p=128), tok_x
                         ).then_inc(early_stored, 16)
            store_xn2(last)
            store_x2(last)

        @block.gpsimd
        def _(pool):
            for i, c in enumerate(ON_GPSIMD):
                n = PROJ[c][3]
                full, rest, _ = SPLIT[c % SPLIT_BUFS]
                pool.wait_ge(part1_ready, c + 1)
                pool.tensor_tensor(out=rest[:, 0:n], in0=full[:, 0:n], in1=part(c, 0, n),
                                   op=ALU.subtract).then_inc(split_g, 1)
                pool.wait_ge(part2_ready, i + 1)
                pool.tensor_tensor(out=part(c, 2, n), in0=rest[:, 0:n], in1=part(c, 1, n),
                                   op=ALU.subtract).then_inc(split_g, 1)
            pool.wait_ge(b2_scaled, 1)
            for t in range(T // 128):
                if t == 0:
                    pool.wait_ge(ln_out, T // 128)
                pool.tensor_tensor(out=x_in[:, t, :], in0=x_in[:, t, :], in1=b2_sb[:, :],
                                   op=ALU.add).then_inc(x_biased, 1)
            def gather(pairs, into, sems, table, index, rows, count):
                for a in pairs:
                    if index is token_slot:
                        pool.wait_ge(token_in[a], count)
                    pool.indirect_dma_start(into(a), None, table, bass.IndirectOffsetOnAxis(index[:, a:a + 1], 0),
                                            bounds_check=rows - 1).then_inc(sems[a], 16)

            def id_of(a):
                return token_slot[:, a:a + 1]

            def row_of(a):
                return tok_x[:, a, :]

            pool.wait_ge(place_in, 1)
            pool.wait_ge(cand_id_stored, 16)
            gather(range(PAIRS), id_of, token_in, cand_id_scr, place_slot, EX * NC * TOP, 0)
            pool.wait_ge(xn2_free, 16 * (NB - 1) + 1)
            gather(range(PAIRS), row_of, x_gathered, xn2_scr, token_slot, T - QB, 16)
            pool.wait_ge(early_stored, 32)
            pool.wait_ge(xn2_free, 16 * NB + 1)
            pool.wait_ge(place_in, 2)
            for pairs in GROUPS:
                gather(pairs, row_of, x_gathered, row_table, place_slot, LAST0 + QB, 0)
                gather(pairs, id_of, token_in, id_table, place_slot, LAST0 + QB, 0)
            pool.wait_ge(x2_free, 16 * NB + 1)
            pool.wait_ge(odd_zero, 16)
            for g, pairs in enumerate(GROUPS):
                pool.wait_ge(odd_ready, g + 1)
                for a in pairs:
                    pool.wait_ge(y_ready, a + 1)
                    for h, (into, token) in enumerate(((out, token_slot), (odd_sum, token_odd))):
                        if a:
                            pool.wait_ge(scattered[h], 16 * a)
                        pool.indirect_dma_start(into, bass.IndirectOffsetOnAxis(token[0:TOP, a:a + 1], 0),
                                                y_out[h * TOP:(h + 1) * TOP, a, :], None, compute_op=ALU.add,
                                                bounds_check=T - 1).then_inc(scattered[h], 16)
            for h in range(2):
                pool.wait_ge(scattered[h], 16 * PAIRS)
            pool.dma_start(out.rearrange("(p t) d -> p (t d)", p=256), odd_sum.rearrange("(p t) d -> p (t d)", p=256),
                           accum_op=ALU.add, max_dma_last_dim=8 * D * 4).then_inc(merged, 16)
            pool.wait_ge(merged, 16)

        @block.scalar
        def _(act):
            act.wait_ge(eps_ready, 1)

            def block_std(b):
                act.wait_ge(ln_mean, QT * (b + 1))
                tiles = slice(b * QT, (b + 1) * QT)
                act.activation(std[:, tiles], moments[:, tiles, 1], ACT.Sqrt, bias=eps[:, :]).then_inc(ln_std, 1)

            def transposed_x(b):
                for k in range(2):
                    act.wait_ge(xt_filled, 2 * b + k + 1)
                    act.activation(xn_tv[:, k, b * QB:(b + 1) * QB], (ps_m if k == 0 else ps_v)[:, :],
                                   ACT.Copy).then_inc(xt_free, 1)

            def projected(c):
                kind, m, c0, n = PROJ[c]
                full = SPLIT[c % SPLIT_BUFS][0]
                fill = FILLS.index(("proj", c))
                act.wait_ge(proj_filled, fill + 1)
                if c >= SPLIT_BUFS:
                    act.wait_ge(stored[c - SPLIT_BUFS], 16)
                act.activation(full[:, 0:n], ps_s[:, fill % RING, 0:n], ACT.Identity,
                               bias=bqk[:, 0 if kind == "q" else 1, m:m + 1]).then_inc(proj_free, 1)
                act.wait_ge(proj_free, fill + 1)
                act.activation(part(c, 0, n), full[:, 0:n], ACT.Copy).then_inc(part1_ready, 1)

            def second_part(c):
                n = PROJ[c][3]
                act.wait_ge(split_g, 2 * ON_GPSIMD.index(c) + 1)
                act.activation(part(c, 1, n), SPLIT[c % SPLIT_BUFS][1][:, 0:n], ACT.Copy).then_inc(part2_ready, 1)

            def values(v):
                keys = 128 if v < KT - 1 else KLAST
                fill = FILLS.index(("v", v))
                act.wait_ge(proj_filled, fill + 1)
                if v == 0:
                    act.wait_ge(v_ones, NG)
                for g in range(NG):
                    cols = slice(g * HG * DH, (g + 1) * HG * DH)
                    last = act.activation(v_cols[g][0:keys, v, :, 0:DH],
                                          ps_s[0:keys, fill % RING, cols].rearrange("p (h d) -> p h d", h=HG),
                                          ACT.Copy)
                last.then_inc(proj_free, 1)

            act.wait_ge(gates_in, 16)
            act.activation(gate[:, :], gate_in[:, :], ACT.Tanh).then_inc(gates_ready, 1)
            act.wait_ge(ctx_in, 64)
            waiting = []
            for what, i in [u[:2] for u in PROLOGUE if u[0] != "max" and u[2]]:
                ready, waiting = waiting, []
                if what == "proj":
                    projected(i)
                    if i == 0:
                        block_std(0)
                    if i in ON_GPSIMD:
                        waiting = [i]
                elif what == "xt":
                    transposed_x(i)
                else:
                    values(i)
                    if i == KT - 4:
                        for b in range(1, NB):
                            block_std(b)
                for c in ready:
                    second_part(c)
            for c in waiting:
                second_part(c)
            for c in range(NPROJ - SPLIT_BUFS, NPROJ):
                if c % SPLIT_BUFS not in (2, 3):
                    act.wait_ge(stored[c], 16)

            act.wait_ge(mlp_in, 16 * LATE_LOADS)

            def unit(s, name):
                b = Step(s.n0 - NG, s.r)
                ps_m = bank(s, name)
                if name.startswith("w1_"):
                    m = int(name[3])
                    wait(act, spare_filled, b.use(name) + 1)
                    act.activation(hidden[:, m, :], ps_m[:, :], ACT.Relu,
                                   bias=b1_sb[:, m:m + 1]).then_inc(spare_free, 1)
                elif name.startswith("tr"):
                    wait(act, spare_filled, b.use(name) + 1)
                    act.activation(xn2_t[:, int(name[2]), :], ps_m[:, :], ACT.Copy).then_inc(spare_free, 1)
                elif name == "lg":
                    wait(act, spare_filled, b.use(name) + 1)
                    if s.n0 == STEPS:
                        act.activation(finalists[:, TOP:TOP + QB], ps_m[0:EX, :], ACT.Identity,
                                       bias=bg_sb[:, :]).then_inc(last_logits, 1)
                    act.activation(logits[:, bass.ds(b.block(scale=QB), QB)], ps_m[0:EX, :], ACT.Identity,
                                   bias=bg_sb[:, :]).then_inc(spare_free, 1)

            def router_std(b):
                wait(act, ln_mean, b.block(1, QT) + NB * QT)
                act.activation(std[:, 0:QT], moments[:, 0:QT, 1], ACT.Sqrt, bias=eps[:, :]).then_inc(ln_std, 1)

            def pv_copy(s):
                wait(act, pv_done, s.count(KT, KT))
                if s.n0 >= 2:
                    wait(act, att_moved[s.g % 2], s.halves(ATT_DMAS))
                    wait(act, den_moved[s.g % 2], s.halves(16))
                act.activation(pv_raw[:, s.g % 2, :], ps_v[:, :], ACT.Copy).then_inc(pv_out, 1)

            def step(s):
                units = dict()
                for kt, name in plan(s.n0):
                    units.setdefault(kt, []).append(name)
                for kt in range(KT):
                    keys = 128 if kt < KT - 1 else KLAST
                    for h in range(HG):
                        j = HG * kt + h
                        wait(act, scores_ready, s.count(TILES, j + 1))
                        if h == 0 and s.n0 * KT + kt >= 2:
                            wait(act, pv_done, s.count(KT, kt - 1))
                        act.activation(probs[0:keys, (s.g * KT + kt) % 2, h, :], score_bank(s, j)[0:keys, :], ACT.Exp,
                                       scale=SCALE).then_inc(exp_done, 1)
                    if kt == 0 and s.n0 >= 1:
                        pv_copy(s.after(-1))
                    if kt == 2 and s.n0 > NG and s.g == 1:
                        router_std(Step(s.n0 - NG, s.r))
                    for name in units.get(kt, []):
                        unit(s, name)

            run_steps(act, step)
            last = Step(STEPS - 1)
            pv_copy(last)
            past = Step(STEPS)
            for _, name in MLP_UNITS:
                unit(past, name)
            router_std(last)
            for _, name in LN_UNITS:
                unit(past, name)

            act.wait_ge(negtop_ready, 1)
            act.wait_ge(spare_free, len(ORDER))
            act.activation(xn_t[0:EX, 0:T], logits[:, :], ACT.Exp, bias=neg_top,
                           accum_out=exp_sum).then_inc(sum_ready, 1)
            act.wait_ge(place_ready, 2)
            act.activation(weight[:, :], top_v[:, :], ACT.Exp, bias=neg_top).then_inc(top_exp, 1)
            for a, l in RELUS:
                act.wait_ge(l_filled, ITEMS.index((a, l)) + 1)
                act.activation(h_out[:, a, :], ps_l[a % 3][:, 0:D], ACT.Relu,
                               bias=eb_sb[:, l, a:a + 1]).then_inc(relu_done, 1)

        @block.vector
        def _(dve):
            dve.memset(zeros[:, :], 0.0).then_inc(zeros_ready, 1)
            dve.memset(eps[:, :], EPS).then_inc(eps_ready, 1)

            def moments_of(src, base, t0=0):
                for t in range(QT):
                    dve.bn_stats(stats[:, t0 + t, :], src[:, t, :]).then_inc(ln_stat, 1)
                aggregate(base, t0)

            def aggregate(base, t0=0):
                wait(dve, ln_stat, base + QT)
                if not isinstance(base, int):
                    dve.memset(carrier[:, 0:1], 0.0)
                for t in range(QT):
                    dve.bn_aggr(moments[:, t0 + t, :], stats[:, t0 + t, :]).then_inc(ln_mean, 1)

            def normalise(src, blocks_before, t0=0, tiles=range(QT)):
                if 0 in tiles:
                    wait(dve, ln_std, blocks_before + 1)
                    dve.reciprocal(rstd[:, t0:t0 + QT], std[:, t0:t0 + QT]).then_inc(ln_rstd, 1)
                    wait(dve, ln_rstd, blocks_before + 1)
                for t in tiles:
                    dve.tensor_scalar(xn2[:, t, :], src[:, t, :], moments[:, t0 + t, 0:1], rstd[:, t0 + t:t0 + t + 1],
                                      ALU.subtract, ALU.mult).then_inc(ln_out, 1)

            def split(c):
                n, i = PROJ[c][3], ON_VECTOR.index(c)
                full, rest, _ = SPLIT[c % SPLIT_BUFS]
                dve.wait_ge(part1_ready, c + 1)
                dve.tensor_tensor(out=rest[:, 0:n], in0=full[:, 0:n], in1=part(c, 0, n),
                                  op=ALU.subtract).then_inc(split_v, 1)
                dve.wait_ge(split_v, 3 * i + 1)
                dve.tensor_copy(part(c, 1, n), rest[:, 0:n]).then_inc(split_v, 1)
                dve.wait_ge(split_v, 3 * i + 2)
                dve.tensor_tensor(out=part(c, 2, n), in0=rest[:, 0:n], in1=part(c, 1, n),
                                  op=ALU.subtract).then_inc(split_v, 1)

            def x_moments(b):
                dve.wait_ge(x_loaded[b], 16)
                moments_of(x_in[:, b * QT:(b + 1) * QT, :], QT * b, QT * b)

            def x_normal(b):
                if b:
                    dve.wait_ge(xt_filled, 2 * b)
                dve.wait_ge(ln_mean, QT * (b + 1))
                normalise(x_in[:, b * QT:(b + 1) * QT, :], b, QT * b)

            dve.memset(carrier[:, 1:2], 0.0).then_inc(x2_free, 1)
            dve.memset(carrier[:, 2:3], 0.0).then_inc(xn2_free, 1)
            dve.memset(rden[:, :], 0.0).then_inc(rden_zero, 1)
            for g in range(NG):
                dve.memset(v_cols[g][:, :, :, DH:DH + 1], 1.0).then_inc(v_ones, 1)
            x_moments(0)
            split(0)
            x_normal(0)
            for c in ON_VECTOR[1:5]:
                split(c)
            for b in range(1, NB):
                x_moments(b)

            def row_max(s, t, h, c):
                g_local = (t * HG + h) * 4 + c
                if g_local == 0 and s.n0 >= 2:
                    wait(dve, neg_ready, s.count(1, -1))
                wait(dve, a_filled, s.count(ACH, g_local + 1))
                col = (h * QT + t) * 4 + c
                dve.reduce_max(cmax[:, s.g % 2, col:col + 1], ps_a[:, ring_bank(g_local, ACH), 0:CHUNKS[c][1]],
                               AX.X).then_inc(a_free, 1)

            def neg_max(s):
                wait(dve, a_free, s.count(ACH, ACH))
                if s.n0 >= 2:
                    wait(dve, spare_filled, Step(s.n0 - 2, s.r).use("neg") + 1)
                dve.tensor_reduce(out=negmax[:, s.g % 2, :],
                                  in_=cmax[:, s.g % 2, :].rearrange("p (u c) -> p u c", c=4),
                                  axis=AX.X, op=ALU.max, negate=True).then_inc(neg_ready, 1)

            def neg_to_parts(s, j):
                if j == 0:
                    wait(dve, spare_filled, s.use("neg") + 1)
                    if s.n0 >= 1:
                        wait(dve, neg_rows, s.count(NEG_DMAS))
                    dve.tensor_copy(neg_parts[:, 0, :], ps_m[0:HG * QT, 0:128]).then_inc(neg_split, 1)
                if j == 1:
                    wait(dve, neg_split, s.count(3, 1))
                    dve.tensor_tensor(out=neg_rest[:, :], in0=ps_m[0:HG * QT, 0:128], in1=neg_parts[:, 0, :],
                                      op=ALU.subtract).then_inc(spare_free, 1)
                if j == 2:
                    wait(dve, spare_free, s.use("neg") + 1)
                    dve.tensor_copy(neg_parts[:, 1, :], neg_rest[:, :]).then_inc(neg_split, 1)
                if j == 3:
                    wait(dve, neg_split, s.count(3, 2))
                    dve.tensor_tensor(out=neg_parts[:, 2, :], in0=neg_rest[:, :], in1=neg_parts[:, 1, :],
                                      op=ALU.subtract).then_inc(neg_split, 1)

            def unit(s, name):
                b = Step(s.n0 - NG, s.r)
                ps_m = bank(s, name)
                if name.startswith("bc"):
                    k = int(name[2])
                    if k == 0:
                        for parity in range(2):
                            wait(dve, att_moved[parity], b.block(1, NG // 2 * ATT_DMAS))
                    wait(dve, spare_filled, b.use(name) + 1)
                    dve.tensor_tensor(out=att_t[:, k, :], in0=ps_m[:, :], in1=att_raw[:, k, :],
                                      op=ALU.mult).then_inc(spare_free, 1)
                elif name.startswith("w2_"):
                    half = int(name[3])
                    if half == 0:
                        wait(dve, x2_free, b.block(scale=16) + 1)
                        dve.wait_ge(x_biased, T // 128)
                    wait(dve, spare_filled, b.use(name) + 1)
                    tiles = slice(2 * half, 2 * half + 2)
                    dve.scalar_tensor_tensor(out=x2[:, tiles, :], in0=ps_m.rearrange("p (t d) -> p t d", t=2),
                                             scalar=gate[:, 0:1],
                                             in1=x_in[:, bass.ds(b.block(scale=QT) + 2 * half, 2), :],
                                             op0=ALU.mult, op1=ALU.add).then_inc(spare_free, 1)

            def denominators(b):
                for parity in range(2):
                    wait(dve, den_moved[parity], b.block(1, NG // 2 * 16))
                dve.reciprocal(den_inv[:, :], den[:, :]).then_inc(den_inverted, 1)

            def router_stats(b, half):
                wait(dve, spare_free, b.use(f"w2_{half}") + 1)
                if half == 0:
                    wait(dve, ln_out, b.block(0, QT) + NB * QT)
                    wait(dve, ln_mean, b.block(0, QT) + NB * QT)
                for t in (2 * half, 2 * half + 1):
                    dve.bn_stats(stats[:, t, :], x2[:, t, :]).then_inc(ln_stat, 1)
                if half:
                    aggregate(b.block(0, QT) + NB * QT)

            def router_norm(b, half):
                if half == 0:
                    wait(dve, xn2_free, b.block(scale=16) + 1)
                    wait(dve, ln_mean, b.block(1, QT) + NB * QT)
                normalise(x2[:, :, :], b.block() + NB, tiles=range(2 * half, 2 * half + 2))

            def between(s, kt):
                prev = Step(s.n0 - NG, s.r)
                if s.n0 >= NG and s.g == 0 and kt == 2:
                    denominators(prev)
                if s.n0 > NG and s.g == 1:
                    for half in range(2):
                        if kt == half:
                            router_stats(prev, half)
                        if kt == 3 + half:
                            router_norm(prev, half)
                for at, name in plan(s.n0):
                    if at == kt:
                        unit(s, name)

            def step(s):
                chunks = row_max_chunks(s.n0)
                neg_from = FIRST_CHUNK[NEG_AT] + HG
                for kt in range(KT):
                    first, after = (min(c, len(chunks)) for c in FIRST_CHUNK[kt:kt + 2])
                    for i in range(first, after):
                        if i == first + HG:
                            between(s, kt)
                        ahead, t, h, c = chunks[i]
                        row_max(s.after(ahead), t, h, c)
                        if (t, h, c) == (QT - 1, HG - 1, 3):
                            neg_max(s.after(ahead))
                        if neg_from <= i < neg_from + 4:
                            neg_to_parts(s.after(1), i - neg_from)
                    if after - first <= HG:
                        between(s, kt)
                    if kt == NEG_AT and s.n0 == STEPS - 2:
                        for j in range(4):
                            neg_to_parts(s.after(1), j)

            for what, i, *_ in PROLOGUE_DVE:
                if what == "xt":
                    x_normal(i)
                else:
                    q, h, c = i
                    row_max(Step(q // QT), q % QT, h, c)
                    if i == (QT - 1, HG - 1, 3):
                        neg_max(Step(0))
                    if i == (QT, 1, 0):
                        for j in range(4):
                            neg_to_parts(Step(0), j)
            dve.wait_ge(mlp_in, 16 * LATE_LOADS)
            dve.wait_ge(gates_ready, 1)
            dve.tensor_scalar(b2_sb[:, :], b2_sb[:, :], gate[:, 0:1], None, ALU.mult).then_inc(b2_scaled, 1)
            run_steps(dve, step)

            def top_rounds(values, places, src, done):
                for k in range(TOP // 8):
                    top8 = values[:, 8 * k:8 * k + 8]
                    if k:
                        dve.wait_ge(done, 3 * k)
                    dve.max(top8, src).then_inc(done, 1)
                    dve.wait_ge(done, 3 * k + 1)
                    if k == 0 and done is top_step:
                        dve.tensor_scalar(neg_top, top_v[:, 0:1], -1.0, None, ALU.mult).then_inc(negtop_ready, 1)
                    dve.max_index(places[:, 8 * k:8 * k + 8], top8, src).then_inc(done, 1)
                    dve.wait_ge(done, 3 * k + 2)
                    dve.match_replace(src, top8, src, -3e38).then_inc(done, 1)
                dve.wait_ge(done, 3 * TOP // 8)

            dve.wait_ge(chunk_in, 16)
            top_rounds(cand, cand_pos, chunk_logits, cand_ready)
            dve.tensor_scalar(cand_id, cand_pos, off[0:EX * NC, 0:1], None, ALU.add).then_inc(cand_ready, 1)
            dve.wait_ge(cand_e_in, 16)
            top_rounds(finalists[:, 0:TOP], early_pos, cand_e, early_step)
            dve.tensor_scalar(place[:, :], early_pos[:, :], off[0:EX, 1:2], None, ALU.add).then_inc(place_ready, 1)
            dve.wait_ge(slots_filled, 1)
            dve.tensor_copy(place_slot[:, :], slots[:, 0:EX // 2]).then_inc(place_in, 1)

            last, past = Step(STEPS - 1), Step(STEPS)
            denominators(last)
            for _, name in MLP_UNITS:
                unit(past, name)
                if name.startswith("w2_"):
                    router_stats(last, int(name[3]))
            for half in range(2):
                router_norm(last, half)

            dve.wait_ge(last_logits, 1)
            top_rounds(top_v, top_pos, finalists[:, :], top_step)
            dve.tensor_scalar(place_tmp[:, 0, :], top_pos[:, :], float(EX // 2 - 1), off[0:EX, 2:3],
                              ALU.mult, ALU.add).then_inc(top_step, 1)
            dve.wait_ge(top_step, 25)
            dve.scalar_tensor_tensor(out=place_tmp[:, 1, :], in0=top_pos[:, :], scalar=float(TOP),
                                     in1=place_tmp[:, 0, :], op0=ALU.is_lt, op1=ALU.mult).then_inc(top_step, 1)
            dve.wait_ge(top_step, 26)
            dve.scalar_tensor_tensor(out=place[:, :], in0=top_pos[:, :], scalar=float(LAST0 - TOP),
                                     in1=place_tmp[:, 1, :], op0=ALU.add, op1=ALU.add).then_inc(place_ready, 1)
            dve.wait_ge(slots_filled, 2)
            for a in range(EX // 2):
                dve.wait_ge(x_gathered[a], 16)
            dve.tensor_copy(place_slot[:, :], slots[:, 0:EX // 2]).then_inc(place_in, 1)
            dve.wait_ge(sum_ready, 1)
            dve.reciprocal(exp_rsum, exp_sum).then_inc(weight_ready, 1)
            dve.wait_ge(weight_ready, 1)
            dve.wait_ge(top_exp, 1)
            dve.tensor_scalar(weight[:, :], weight[:, :], exp_rsum, gate[0:EX, 1:2], ALU.mult, ALU.mult
                              ).then_inc(weight_ready, 1)
            dve.wait_ge(slots_filled, 3)
            dve.tensor_copy(weight_slot[:, :], slots[:, EX // 2:EX]).then_inc(weight_in, 1)
            def copy_transposed(i):
                a, l = ITEMS[i]
                dve.wait_ge(t_filled, i + 1)
                if i == 0:
                    dve.wait_ge(sum_ready, 1)
                dve.tensor_copy(h_in[:, a, :, :], ps_t[a % 3][:, 0:2 * 128].rearrange("p (k n) -> p k n", k=2)
                                ).then_inc(t_free, 1)

            copy_transposed(0)
            for i, (a, l) in enumerate(ITEMS):
                g = [a in pairs for pairs in GROUPS].index(True)
                if i + 1 < len(ITEMS):
                    copy_transposed(i + 1)
                if (a, l) == (GROUPS[g][-1], 1):
                    for b in GROUPS[g]:
                        dve.wait_ge(token_in[b], 32)
                    cols = slice(GROUPS[g][0], GROUPS[g][-1] + 1)
                    dve.tensor_copy(token_f[:, cols], token_slot[:, cols]).then_inc(token_f_ready, 1)
                if l == 2:
                    if a == GROUPS[g][0]:
                        dve.wait_ge(odd_filled, g + 1)
                        dve.tensor_copy(token_odd[:, cols], ps_m[0:TOP, cols]).then_inc(odd_ready, 1)
                    dve.wait_ge(l_filled, i + 1)
                    if a == 0:
                        dve.wait_ge(weight_in, 1)
                    dve.tensor_scalar(y_out[:, a, :], ps_l[a % 3][:, 0:D], eb_sb[:, 2, a:a + 1],
                                      weight_slot[:, a:a + 1], ALU.add, ALU.mult).then_inc(y_ready, 1)

        @block.tensor
        def _(pe):
            def stay_awake(count):
                for _ in range(count):
                    pe.matmul(ps_s[:, 0, 0:D], zeros[:, 0:128], zeros[:, :], start=True, stop=True)

            def project(c, k):
                kind, m, c0, n = PROJ[c]
                fill = FILLS.index(("proj", c))
                if k == 0 and fill >= RING:
                    pe.wait_ge(proj_free, fill - RING + 1)
                w, src = (wk_sb, ctx_sb) if kind == "k" else (wq_sb, xn_tv)
                rows = CH if kind == "k" else 128
                if k == 0 and kind == "q":
                    pe.wait_ge(q_in, 16)
                    pe.wait_ge(xt_free, 2 * (c0 // QB) + 2)
                last = pe.matmul(ps_s[:, fill % RING, 0:n], w[0:rows, k, m * 128:(m + 1) * 128],
                                 src[0:rows, k, c0:c0 + n], start=k == 0, stop=k == 1)
                if k:
                    last.then_inc(proj_filled, 1)

            def transpose_x(b, k):
                pe.wait_ge(ln_out, QT * (b + 1))
                if b:
                    pe.wait_ge(xt_free, 2 * b + k - 1)
                for t in range(QT):
                    last = pe.transpose((ps_m if k == 0 else ps_v)[:, t * 128:(t + 1) * 128],
                                        xn2[:, t, k * 128:(k + 1) * 128], ident[:, :])
                last.then_inc(xt_filled, 1)

            def values(v, k):
                keys = 128 if v < KT - 1 else KLAST
                fill = FILLS.index(("v", v))
                if k == 0:
                    pe.wait_ge(v_in, 48)
                    pe.wait_ge(proj_free, fill - RING + 1)
                rows = CH + k
                last = pe.matmul(ps_s[0:keys, fill % RING, 0:D], ctx_sb[0:rows, k, v * 128:v * 128 + keys],
                                 wv_sb[0:rows, k, :], start=k == 0, stop=k == 1)
                if k:
                    last.then_inc(proj_filled, 1)

            def row_max(s, t, h, c):
                g_local = (t * HG + h) * 4 + c
                if g_local == 0:
                    wait(pe, q_loaded[s.g], s.block(1, 3 * 16))
                    if s.n0 < NG:
                        pe.wait_ge(k_relaid[s.n0], 3 * 16)
                if s.n0 or g_local >= RING:
                    wait(pe, a_free, s.count(ACH, ring_wait(g_local, ACH)))
                c0, n = CHUNKS[c]
                pe.matmul(ps_a[:, ring_bank(g_local, ACH), 0:n], q_rows[s.g][0:PARTS, h, t * 128:(t + 1) * 128],
                          k_rows[s.g][0:PARTS, h, c0:c0 + n], start=True, stop=True).then_inc(a_filled, 1)

            def transpose_neg(s):
                wait(pe, neg_ready, s.count(1, 1))
                if s.n0:
                    wait(pe, spare_free, s.use("neg"))
                else:
                    pe.wait_ge(xt_free, 2 * NB)
                pe.transpose(ps_m[0:HG * QT, 0:128], negmax[:, s.g % 2, :], ident[:, :]).then_inc(spare_filled, 1)

            def unit(s, name):
                b = Step(s.n0 - NG, s.r)
                ps_m = bank(s, name)
                if name == "neg":
                    return transpose_neg(s.after(1))
                wait(pe, spare_free, b.use(name if s.n0 < STEPS else first_of(name)))
                if name.startswith("bc"):
                    if name == "bc0":
                        wait(pe, rden_ready, b.block(1, 16))
                    last = pe.matmul(ps_m[:, :], spread[:, int(name[2]), :], rden[:, :], start=True, stop=True)
                elif name.startswith("w1_"):
                    m = int(name[3])
                    for k in range(2):
                        last = pe.matmul(ps_m[:, :], w1_sb[:, k, m * 128:(m + 1) * 128], att_t[:, k, :],
                                         start=k == 0, stop=k == 1)
                elif name.startswith("w2_"):
                    for t in range(2):
                        rows = slice((2 * int(name[3]) + t) * 128, (2 * int(name[3]) + t + 1) * 128)
                        for k in range(4):
                            last = pe.matmul(ps_m[:, t * D:(t + 1) * D], hidden[:, k, rows], w2_sb[:, k, :],
                                             start=k == 0, stop=k == 3)
                elif name.startswith("tr"):
                    k = int(name[2])
                    wait(pe, ln_out, b.block(1, QT) + NB * QT)
                    for t in range(QT):
                        last = pe.transpose(ps_m[:, t * 128:(t + 1) * 128], xn2[:, t, k * 128:(k + 1) * 128],
                                            ident[:, :])
                elif name == "lg":
                    for k in range(2):
                        last = pe.matmul(ps_m[0:EX, :], wg_sb[:, k, :], xn2_t[:, k, :], start=k == 0, stop=k == 1)
                last.then_inc(spare_filled, 1)

            def times_v(s, kt):
                keys = 128 if kt < KT - 1 else KLAST
                wait(pe, exp_done, s.count(TILES, HG * (kt + 1)))
                if kt == 0 and s.n0:
                    wait(pe, pv_out, s.count(1))
                for h in range(HG):
                    last = pe.matmul(ps_v[32 * h:32 * h + DH + 1, :], v_cols[s.g][0:keys, kt, h, :],
                                     probs[0:keys, (s.g * KT + kt) % 2, h, :], start=kt == 0, stop=kt == KT - 1)
                last.then_inc(pv_done, 1)

            def step(s):
                chunks = row_max_chunks(s.n0)
                todo = iter(chunks)

                def next_chunks(count):
                    for _, (ahead, t, h, c) in zip(range(count), todo):
                        row_max(s.after(ahead), t, h, c)

                for kt in range(KT):
                    keys = 128 if kt < KT - 1 else KLAST
                    for h in range(HG):
                        j = HG * kt + h
                        if s.n0 == STEPS - 1 and RING <= j < 2 * RING:
                            wait(pe, a_free, s.count(ACH, ACH))
                        elif s.n0 * TILES + j >= RING:
                            read = j - 2 * RING + 1 if s.n0 == STEPS - 1 and j >= RING else ring_wait(j, TILES)
                            wait(pe, exp_done, s.count(TILES, read))
                        if kt == 0 and h == 0:
                            wait(pe, neg_rows, s.count(NEG_DMAS, NEG_DMAS))
                        pe.matmul(score_bank(s, j)[0:keys, :], k_rows[s.g][0:PARTS + 3, h, kt * 128:kt * 128 + keys],
                                  q_rows[s.g][0:PARTS + 3, h, :], start=True, stop=True).then_inc(scores_ready, 1)
                        next_chunks(1)
                    if kt:
                        times_v(s, kt - 1)
                    elif s.n0:
                        times_v(s.after(-1), KT - 1)
                    for at, name in plan(s.n0):
                        if at == kt:
                            unit(s, name)
                    next_chunks(TILE_CHUNKS[kt] - HG)

            pe.wait_ge(zeros_ready, 1)
            stay_awake(7)
            pe.wait_ge(ctx_in, 64)
            pe.wait_ge(ident_in, 16)
            for what, i, *k in PROLOGUE:
                if what == "proj":
                    project(i, *k)
                elif what == "xt":
                    transpose_x(i, *k)
                elif what == "v":
                    values(i, *k)
                else:
                    q, h, c = i
                    row_max(Step(q // QT), q % QT, h, c)
                    if i == (QT, 0, 2):
                        transpose_neg(Step(0))
            pe.wait_ge(proj_free, NPROJ + KT)
            pe.wait_ge(ones_in, 16 * NG)
            pe.wait_ge(mlp_in, 16 * LATE_LOADS)
            run_steps(pe, step)

            last, past = Step(STEPS - 1), Step(STEPS)
            times_v(last, KT - 1)

            def to_slots(src, col):
                pairs = ident[0:EX, 0:EX].rearrange("p (a h) -> p h a", h=2)
                for h in range(2):
                    last = pe.matmul(slots[h * TOP:(h + 1) * TOP, col:col + EX // 2], src[:, :], pairs[:, h, :],
                                     start=True, stop=True)
                last.then_inc(slots_filled, 1)

            stay_awake(4)
            pe.wait_ge(place_ready, 1)
            to_slots(place, 0)
            stay_awake(8)
            for _, name in MLP_UNITS:
                unit(past, name)
            stay_awake(10)
            for _, name in LN_UNITS:
                unit(past, name)

            pe.wait_ge(spare_free, len(ORDER))
            pe.wait_ge(top_step, 15)
            stay_awake(10)
            pe.wait_ge(place_ready, 2)
            to_slots(place, 0)
            pe.wait_ge(weight_ready, 2)
            to_slots(weight, EX // 2)
            stay_awake(5)

            def transpose_rows(i):
                a, l = ITEMS[i]
                if l == 0:
                    pe.wait_ge(x_gathered[a], 32)
                    src = tok_x[:, a, :]
                else:
                    pe.wait_ge(relu_done, RELUS.index((a, l - 1)) + 1)
                    src = h_out[:, a, :]
                if l:
                    pe.wait_ge(t_free, ITEMS.index((a, l - 1)) + 1)
                elif a >= 3:
                    pe.wait_ge(t_free, ITEMS.index((a - 3, 2)) + 1)
                for k in range(2):
                    last = pe.transpose(ps_t[a % 3][:, k * 128:(k + 1) * 128], src[:, k * 128:(k + 1) * 128],
                                        ident[:, :])
                last.then_inc(t_filled, 1)

            transpose_rows(0)
            for i, (a, l) in enumerate(ITEMS):
                g = [a in pairs for pairs in GROUPS].index(True)
                if i + 1 < len(ITEMS):
                    transpose_rows(i + 1)
                if a == 0:
                    pe.wait_ge(w_in[l], 16 * expert_dmas(l))
                pe.wait_ge(t_free, i + 1)
                if l:
                    pe.wait_ge(relu_done, RELUS.index((a, l - 1)) + 1)
                elif a >= 3:
                    pe.wait_ge(y_ready, OUTS.index((a - 3, 2)) + 1)
                for k in range(2):
                    for h in range(2):
                        last = pe.matmul(ps_l[a % 3][h * TOP:(h + 1) * TOP, 0:D], h_in[:, a, k, h * TOP:(h + 1) * TOP],
                                         w_exp[:, l, 2 * a + h, k, :], start=k == 0, stop=k == 1)
                last.then_inc(l_filled, 1)
                if (a, l) == (GROUPS[g][-1], 1):
                    pe.wait_ge(token_f_ready, g + 1)
                    cols = slice(GROUPS[g][0], GROUPS[g][-1] + 1)
                    pe.matmul(ps_m[0:TOP, cols], ident[:, TOP:2 * TOP], token_f[:, cols],
                              start=True, stop=True).then_inc(odd_filled, 1)


def prologue_order():
    def halves(what, i):
        return [(what, i, 0), (what, i, 1)]

    order = sum((halves("proj", c) for c in range(4)), []) + halves("xt", 0) + halves("proj", 4) + halves("proj", 5)
    order += sum((halves("v", v) for v in range(KT)), [])
    rest = sum((halves("proj", c) for c in range(6, 10)), [])
    for b in range(1, NB):
        rest += halves("xt", b) + halves("proj", 8 + 2 * b) + halves("proj", 9 + 2 * b)
    cost = {"proj": 2.0, "xt": 1.5}
    chunks = [("max", (q, h, c)) for q in range(QT + LEAD) for h in range(HG) for c in range(4)]
    total, spent = sum(cost[u[0]] for u in rest), 0.0
    for i, chunk in enumerate(chunks):
        order.append(chunk)
        while rest and spent < (i + 1) / (SPREAD * len(chunks)) * total:
            order.append(rest.pop(0))
            spent += cost[order[-1][0]]
    return order + rest


def prologue_order_dve():
    order = [u for u in PROLOGUE if u[0] == "max" or u[0] == "xt" and u[1] and not u[2]]
    for b in range(1, NB):
        at = order.index(("xt", b, 0))
        order.insert(max(0, at - 8), order.pop(at))
    return order


PROLOGUE = prologue_order()
PROLOGUE_DVE = prologue_order_dve()
FILLS = [u[:2] for u in PROLOGUE if u[0] in ("proj", "v") and not u[2]]


def kernel(x, ctx_768, g_xattn, g_ffn, L0_xattn_Wq, L0_xattn_bq, L0_xattn_Wk, L0_xattn_bk, L0_xattn_Wv,
           L0_xattn_bv, L0_xattn_W1, L0_xattn_b1, L0_xattn_W2, L0_xattn_b2, L0_ffn_Wg, L0_ffn_bg, L0_ffn_w1,
           L0_ffn_b1, L0_ffn_w2, L0_ffn_b2, L0_ffn_w3, L0_ffn_b3):
    import ml_dtypes
    import numpy as np
    import concourse.bacc as bacc
    from concourse.bass_utils import run_bass_kernel_spmd

    def d_major(a):
        a = np.asarray(a)
        return a.reshape(-1, 2, HM, DH).transpose(0, 1, 3, 2).reshape(-1, D)

    def rows(a, k):
        return np.asarray(a).reshape(k, 128).T

    head_of_row = np.arange(D).reshape(2, 128) // DH
    arrays = {
        "ident": np.eye(128, dtype=np.float32),
        "spread": (np.arange(128)[:, None, None] == head_of_row).astype(np.float32),
        "ones": np.ones((3, HG * S), ml_dtypes.bfloat16),
        "ones_row": np.ones((1, S), np.float32),
        "offsets": np.array(offsets(), np.float32).T,
        "last_tokens": np.arange(T - QB, T, dtype=np.uint32).reshape(QB, 1),
        "x": np.asarray(x)[0],
        "ctx_t": np.asarray(ctx_768)[0].T,
        "wq": d_major(L0_xattn_Wq),
        "bqk": np.stack([rows(d_major(L0_xattn_bq), 2), rows(d_major(L0_xattn_bk), 2)], axis=1),
        "wk": d_major(L0_xattn_Wk),
        "wv": np.asarray(L0_xattn_Wv),
        "bv": np.asarray(L0_xattn_bv).reshape(1, D),
        "w1": np.asarray(L0_xattn_W1),
        "b1": rows(L0_xattn_b1, 4),
        "w2": np.asarray(L0_xattn_W2),
        "b2": np.broadcast_to(np.asarray(L0_xattn_b2), (128, D)),
        "wg": np.asarray(L0_ffn_Wg),
        "bg": np.asarray(L0_ffn_bg).reshape(EX, 1),
        "gates": np.broadcast_to(np.concatenate([np.asarray(g_xattn), np.asarray(g_ffn)]), (128, 2)),
        "ew1": np.asarray(L0_ffn_w1),
        "ew2": np.asarray(L0_ffn_w2),
        "ew3": np.asarray(L0_ffn_w3),
        "eb": np.stack([np.repeat(np.asarray(b).reshape(EX // 2, 2).T, TOP, axis=0)
                        for b in (L0_ffn_b1, L0_ffn_b2, L0_ffn_b3)], axis=1),
    }
    arrays = {k: np.ascontiguousarray(v) for k, v in arrays.items()}
    nc = bacc.Bacc("TRN2", target_bir_lowering=False, num_devices=1)
    ap = {k: nc.dram_tensor("in_" + k, v.shape, mybir.dt.from_np(v.dtype), kind="ExternalInput").ap()
          for k, v in arrays.items()}
    out = nc.dram_tensor("out", (1, T, D), F32, kind="ExternalOutput").ap()
    flamingo(nc, ap, ap["x"], ap["ctx_t"], ap["wq"], ap["bqk"], ap["wk"], ap["wv"], ap["bv"], ap["w1"], ap["b1"],
             ap["w2"], ap["b2"], ap["wg"], ap["bg"], ap["gates"], (ap["ew1"], ap["ew2"], ap["ew3"]), ap["eb"],
             out.rearrange("o t d -> (o t) d"))
    result = run_bass_kernel_spmd(nc, [{"in_" + k: v for k, v in arrays.items()}], core_ids=[0])
    return result.results[0]["out"]
```
